# Optimizing a Trainium2 kernel written in Bass

```python
import numpy as np
import jax
import jax.numpy as jnp

def _softmax(x, axis=-1):
    return jax.nn.softmax(x, axis=axis)

def _gelu(x):
    return jax.nn.gelu(x, approximate=True)

def _silu(x):
    return jax.nn.silu(x)

def _sigmoid(x):
    return jax.nn.sigmoid(x)

def _layernorm(x, axis=-1, eps=1e-05):
    m = jnp.mean(x, axis=axis, keepdims=True)
    v = jnp.var(x, axis=axis, keepdims=True)
    return (x - m) / jnp.sqrt(v + eps)

def _scatter_add(tgt, idx, src, axis=0):
    return tgt.at[idx].add(src)

def _segment_sum(src, seg, n):
    return jax.ops.segment_sum(src, seg, n)
kernel_name = 'mk_adj_resnorm_d4_adj_r2_2f8759'

def setup_inputs(seed: int=0):
    np.random.seed(seed)
    _w = jnp.asarray

    def _rec_inputs():
        import jax
        import jax.numpy as jnp
        _gk = jax.random.key(seed)
        x = -0.0005207 + 1.001 * jax.random.normal(jax.random.fold_in(_gk, 1), (64, 128, 128), jnp.float32)
        _a = jax.random.bernoulli(jax.random.fold_in(_gk, 2), 0.125, (64, 128, 128))
        _a = jnp.logical_or(_a, jnp.swapaxes(_a, -1, -2))
        _a = jnp.logical_or(_a, jnp.eye(128, dtype=bool))
        _af = _a.astype(jnp.float32)
        _af = _af * jax.random.uniform(jax.random.fold_in(_gk, 3), (64, 128, 128), jnp.float32, 0.05, 1)
        adj = _af
        return (x, adj)
    x, adj = _rec_inputs()

    def _L0_gnn_setup():
        import jax, jax.numpy as jnp
        import numpy as np
        EPS = 1e-06
        key = jax.random.key(seed)
        k_x, k_a, k_w, k_b = jax.random.split(key, 4)
        B, N, Fin, Fout = (8, 1024, 128, 128)
        X = jax.random.normal(k_x, (B, N, Fin), dtype=jnp.float32)
        A = jax.random.uniform(k_a, (B, N, N), dtype=jnp.float32)
        bound = 1.0 / np.sqrt(Fin)
        W = jax.random.uniform(k_w, (Fout, Fin), minval=-bound, maxval=bound, dtype=jnp.float32)
        b = jax.random.uniform(k_b, (Fout,), minval=-bound, maxval=bound, dtype=jnp.float32)
        return {'X': X, 'A': A, 'W': W, 'b': b}
    _L0_gnn_all = _L0_gnn_setup()
    _L0_gnn_in = {k: v for k, v in _L0_gnn_all.items() if k in ('W', 'b')}
    del _L0_gnn_all

    def _L1_gnn_setup():
        import jax, jax.numpy as jnp
        import numpy as np
        B, N, D = (1024, 64, 128)

        def _forward(x, graph, W_ir, b_ir, W_hr, b_hr, W_xr, b_xr, W_iz, b_iz, W_hz, b_hz, W_xz, b_xz, W_im, b_im, W_hm, b_hm, W_xm, b_xm):
            n = x.shape[-2]
            eye = jnp.eye(n, dtype=bool)
            g = jnp.where(eye, jnp.zeros((), x.dtype), graph)
            gIr = jnp.einsum('btj,bjd->btd', g, x @ W_ir + b_ir)
            gIz = jnp.einsum('btj,bjd->btd', g, x @ W_iz + b_iz)
            gIm = jnp.einsum('btj,bjd->btd', g, x @ W_im + b_im)
            xr = x @ W_xr + b_xr
            xz = x @ W_xz + b_xz
            xm = x @ W_xm + b_xm
            seq = jnp.stack([gIr + xr, gIz + xz, gIm + xm], axis=0)
            seq = jnp.moveaxis(seq, 2, 0)

            def step(h, a):
                a_r, a_z, a_m = (a[0], a[1], a[2])
                r = jax.nn.sigmoid(a_r + h @ W_hr + b_hr)
                z = jax.nn.sigmoid(a_z + h @ W_hz + b_hz)
                m = jnp.tanh(a_m + r * (h @ W_hm + b_hm))
                h = (1.0 - z) * m + z * h
                return (h, h)
            h0 = jnp.zeros(x.shape[:-2] + (x.shape[-1],), x.dtype)
            _, out = jax.lax.scan(step, h0, seq)
            out = jnp.moveaxis(out, 0, 1)
            return jax.nn.relu(out)
        key = jax.random.key(seed)
        ks = jax.random.split(key, 12)
        x = jax.random.normal(ks[0], (B, N, D), jnp.float32)
        tril = jnp.tril(jnp.ones((N, N), dtype=bool), k=-1)
        graph = jax.random.uniform(ks[1], (B, N, N), dtype=jnp.float32) * tril
        s = 1.0 / np.sqrt(D)
        inp = {'x': x, 'graph': graph}
        names = ['ir', 'hr', 'xr', 'iz', 'hz', 'xz', 'im', 'hm', 'xm']
        for i, n in enumerate(names):
            kw, kb = jax.random.split(ks[2 + i])
            inp[f'W_{n}'] = jax.random.uniform(kw, (D, D), jnp.float32, minval=-s, maxval=s)
            inp[f'b_{n}'] = jax.random.uniform(kb, (D,), jnp.float32, minval=-s, maxval=s)
        return inp
    _L1_gnn_all = _L1_gnn_setup()
    _L1_gnn_in = {k: v for k, v in _L1_gnn_all.items() if k in ('W_ir', 'b_ir', 'W_hr', 'b_hr', 'W_xr', 'b_xr', 'W_iz', 'b_iz', 'W_hz', 'b_hz', 'W_xz', 'b_xz', 'W_im', 'b_im', 'W_hm', 'b_hm', 'W_xm', 'b_xm')}
    del _L1_gnn_all

    def _L2_gnn_setup():
        import jax, jax.numpy as jnp
        import numpy as np
        BS, N, D_IN, D_OUT = (8, 1024, 128, 128)
        key = jax.random.key(seed)
        k1, k2, k3, k4 = jax.random.split(key, 4)
        x = jax.random.normal(k1, (BS, N, D_IN), dtype=jnp.float32)
        adj = jax.random.uniform(k2, (BS, N, N), dtype=jnp.float32)
        theta = jax.random.normal(k3, (D_IN, D_OUT), dtype=jnp.float32) * (1.0 / np.sqrt(D_OUT))
        bias = jax.random.normal(k4, (D_OUT,), dtype=jnp.float32) * (1.0 / np.sqrt(D_OUT))
        return {'x': x, 'adj': adj, 'theta': theta, 'bias': bias}
    _L2_gnn_all = _L2_gnn_setup()
    _L2_gnn_in = {k: v for k, v in _L2_gnn_all.items() if k in ('theta', 'bias')}
    del _L2_gnn_all

    def _L3_gnn_setup():
        import jax, jax.numpy as jnp
        import numpy as np
        B, N, NAB, NF, NG = (8, 128, 128, 128, 64)
        CUTOFF = 5.0
        LN2 = float(np.log(2.0))

        def ssp(x):
            return jax.nn.softplus(x) - LN2
        key = jax.random.key(seed)
        ks = jax.random.split(key, 12)
        r = jax.random.normal(ks[0], (B, N, NAB), dtype=jnp.float32)
        e = jax.random.uniform(ks[1], (B, N, N), dtype=jnp.float32) * CUTOFF
        A = (jax.random.uniform(ks[2], (B, N, N)) < 0.3).astype(jnp.float32)
        s = 0.05
        W1 = jax.random.normal(ks[3], (NF, NG), dtype=jnp.float32) * s
        b1 = jnp.zeros((NF,), jnp.float32)
        W2 = jax.random.normal(ks[4], (NF, NF), dtype=jnp.float32) * s
        b2 = jnp.zeros((NF,), jnp.float32)
        Wa = jax.random.normal(ks[5], (NF, NAB), dtype=jnp.float32) * s
        Wd1 = jax.random.normal(ks[6], (NAB, NF), dtype=jnp.float32) * s
        bd1 = jnp.zeros((NAB,), jnp.float32)
        Wd2 = jax.random.normal(ks[7], (NAB, NAB), dtype=jnp.float32) * s
        bd2 = jnp.zeros((NAB,), jnp.float32)
        return {'r': r, 'e': e, 'A': A, 'W1': W1, 'b1': b1, 'W2': W2, 'b2': b2, 'Wa': Wa, 'Wd1': Wd1, 'bd1': bd1, 'Wd2': Wd2, 'bd2': bd2}
    _L3_gnn_all = _L3_gnn_setup()
    _L3_gnn_in = {k: v for k, v in _L3_gnn_all.items() if k in ('W1', 'b1', 'W2', 'b2', 'Wa', 'Wd1', 'bd1', 'Wd2', 'bd2')}
    del _L3_gnn_all
    return {'x': x, 'adj': adj, 'L0_gnn_W': _L0_gnn_in['W'], 'L0_gnn_b': _L0_gnn_in['b'], 'L1_gnn_W_ir': _L1_gnn_in['W_ir'], 'L1_gnn_b_ir': _L1_gnn_in['b_ir'], 'L1_gnn_W_hr': _L1_gnn_in['W_hr'], 'L1_gnn_b_hr': _L1_gnn_in['b_hr'], 'L1_gnn_W_xr': _L1_gnn_in['W_xr'], 'L1_gnn_b_xr': _L1_gnn_in['b_xr'], 'L1_gnn_W_iz': _L1_gnn_in['W_iz'], 'L1_gnn_b_iz': _L1_gnn_in['b_iz'], 'L1_gnn_W_hz': _L1_gnn_in['W_hz'], 'L1_gnn_b_hz': _L1_gnn_in['b_hz'], 'L1_gnn_W_xz': _L1_gnn_in['W_xz'], 'L1_gnn_b_xz': _L1_gnn_in['b_xz'], 'L1_gnn_W_im': _L1_gnn_in['W_im'], 'L1_gnn_b_im': _L1_gnn_in['b_im'], 'L1_gnn_W_hm': _L1_gnn_in['W_hm'], 'L1_gnn_b_hm': _L1_gnn_in['b_hm'], 'L1_gnn_W_xm': _L1_gnn_in['W_xm'], 'L1_gnn_b_xm': _L1_gnn_in['b_xm'], 'L2_gnn_theta': _L2_gnn_in['theta'], 'L2_gnn_bias': _L2_gnn_in['bias'], 'L3_gnn_W1': _L3_gnn_in['W1'], 'L3_gnn_b1': _L3_gnn_in['b1'], 'L3_gnn_W2': _L3_gnn_in['W2'], 'L3_gnn_b2': _L3_gnn_in['b2'], 'L3_gnn_Wa': _L3_gnn_in['Wa'], 'L3_gnn_Wd1': _L3_gnn_in['Wd1'], 'L3_gnn_bd1': _L3_gnn_in['bd1'], 'L3_gnn_Wd2': _L3_gnn_in['Wd2'], 'L3_gnn_bd2': _L3_gnn_in['bd2']}

def reference(x, adj, L0_gnn_W, L0_gnn_b, L1_gnn_W_ir, L1_gnn_b_ir, L1_gnn_W_hr, L1_gnn_b_hr, L1_gnn_W_xr, L1_gnn_b_xr, L1_gnn_W_iz, L1_gnn_b_iz, L1_gnn_W_hz, L1_gnn_b_hz, L1_gnn_W_xz, L1_gnn_b_xz, L1_gnn_W_im, L1_gnn_b_im, L1_gnn_W_hm, L1_gnn_b_hm, L1_gnn_W_xm, L1_gnn_b_xm, L2_gnn_theta, L2_gnn_bias, L3_gnn_W1, L3_gnn_b1, L3_gnn_W2, L3_gnn_b2, L3_gnn_Wa, L3_gnn_Wd1, L3_gnn_bd1, L3_gnn_Wd2, L3_gnn_bd2):
    import jax
    import jax.numpy as jnp

    def _L0_gnn_ref(X, A, W, b):
        import jax, jax.numpy as jnp
        import numpy as np
        EPS = 1e-06
        N = A.shape[-1]
        A_hat = A + jnp.eye(N, dtype=A.dtype)
        d_inv_sqrt = (jnp.sum(A_hat, axis=-1) + EPS) ** (-0.5)
        A_norm = d_inv_sqrt[:, :, None] * A_hat * d_inv_sqrt[:, None, :]
        support = jnp.einsum('bnm,bmf->bnf', A_norm, X)
        out = jnp.einsum('bnf,of->bno', support, W) + b
        return jax.nn.relu(out)

    def _L1_gnn_ref(x, graph, W_ir, b_ir, W_hr, b_hr, W_xr, b_xr, W_iz, b_iz, W_hz, b_hz, W_xz, b_xz, W_im, b_im, W_hm, b_hm, W_xm, b_xm):
        import jax, jax.numpy as jnp
        import numpy as np
        B, N, D = (1024, 64, 128)

        def _forward(x, graph, W_ir, b_ir, W_hr, b_hr, W_xr, b_xr, W_iz, b_iz, W_hz, b_hz, W_xz, b_xz, W_im, b_im, W_hm, b_hm, W_xm, b_xm):
            n = x.shape[-2]
            eye = jnp.eye(n, dtype=bool)
            g = jnp.where(eye, jnp.zeros((), x.dtype), graph)
            gIr = jnp.einsum('btj,bjd->btd', g, x @ W_ir + b_ir)
            gIz = jnp.einsum('btj,bjd->btd', g, x @ W_iz + b_iz)
            gIm = jnp.einsum('btj,bjd->btd', g, x @ W_im + b_im)
            xr = x @ W_xr + b_xr
            xz = x @ W_xz + b_xz
            xm = x @ W_xm + b_xm
            seq = jnp.stack([gIr + xr, gIz + xz, gIm + xm], axis=0)
            seq = jnp.moveaxis(seq, 2, 0)

            def step(h, a):
                a_r, a_z, a_m = (a[0], a[1], a[2])
                r = jax.nn.sigmoid(a_r + h @ W_hr + b_hr)
                z = jax.nn.sigmoid(a_z + h @ W_hz + b_hz)
                m = jnp.tanh(a_m + r * (h @ W_hm + b_hm))
                h = (1.0 - z) * m + z * h
                return (h, h)
            h0 = jnp.zeros(x.shape[:-2] + (x.shape[-1],), x.dtype)
            _, out = jax.lax.scan(step, h0, seq)
            out = jnp.moveaxis(out, 0, 1)
            return jax.nn.relu(out)
        return _forward(x, graph, W_ir, b_ir, W_hr, b_hr, W_xr, b_xr, W_iz, b_iz, W_hz, b_hz, W_xz, b_xz, W_im, b_im, W_hm, b_hm, W_xm, b_xm)

    def _L2_gnn_ref(x, adj, theta, bias):
        import jax, jax.numpy as jnp
        import numpy as np
        BS, N, D_IN, D_OUT = (8, 1024, 128, 128)
        n = adj.shape[1]
        adj = adj + jnp.eye(n, dtype=adj.dtype)
        deg = jnp.sum(adj, axis=2)
        d_inv_sqrt = 1.0 / jnp.sqrt(deg)
        adj_norm = adj * d_inv_sqrt[:, :, None] * d_inv_sqrt[:, None, :]
        support = jnp.einsum('bni,io->bno', x, theta)
        out = jnp.einsum('bnm,bmo->bno', adj_norm, support) + bias
        return out

    def _L3_gnn_ref(r, e, A, W1, b1, W2, b2, Wa, Wd1, bd1, Wd2, bd2):
        import jax, jax.numpy as jnp
        import numpy as np
        B, N, NAB, NF, NG = (8, 128, 128, 128, 64)
        CUTOFF = 5.0
        LN2 = float(np.log(2.0))

        def ssp(x):
            return jax.nn.softplus(x) - LN2
        offsets = jnp.linspace(0.0, CUTOFF, NG, dtype=jnp.float32)
        width = offsets[1] - offsets[0]
        coeff = -0.5 / (width * width)
        diff = e[:, :, :, None] - offsets
        g = jnp.exp(coeff * diff * diff)
        h = ssp(jnp.einsum('bijg,fg->bijf', g, W1) + b1)
        Wf = jnp.einsum('bijf,gf->bijg', h, W2) + b2
        rf = jnp.einsum('bjd,fd->bjf', r, Wa)
        Am = A[:, :, :, None]
        Wf = Wf * Am
        y = jnp.einsum('bjf,bijf->bif', rf, Wf * Am)
        y = ssp(jnp.einsum('bif,df->bid', y, Wd1) + bd1)
        y = jnp.einsum('bid,ed->bie', y, Wd2) + bd2
        return y
    x = _layernorm(x + _L0_gnn_ref(x, adj, L0_gnn_W, L0_gnn_b), axis=-1)
    x = _layernorm(x + _L1_gnn_ref(x, adj, L1_gnn_W_ir, L1_gnn_b_ir, L1_gnn_W_hr, L1_gnn_b_hr, L1_gnn_W_xr, L1_gnn_b_xr, L1_gnn_W_iz, L1_gnn_b_iz, L1_gnn_W_hz, L1_gnn_b_hz, L1_gnn_W_xz, L1_gnn_b_xz, L1_gnn_W_im, L1_gnn_b_im, L1_gnn_W_hm, L1_gnn_b_hm, L1_gnn_W_xm, L1_gnn_b_xm), axis=-1)
    x = _layernorm(x + _L2_gnn_ref(x, adj, L2_gnn_theta, L2_gnn_bias), axis=-1)
    x = _layernorm(x + _L3_gnn_ref(x, adj, adj, L3_gnn_W1, L3_gnn_b1, L3_gnn_W2, L3_gnn_b2, L3_gnn_Wa, L3_gnn_Wd1, L3_gnn_bd1, L3_gnn_Wd2, L3_gnn_bd2), axis=-1)
    return x

_drawn_inputs = setup_inputs


def setup_inputs(seed=0):
    import zlib

    import numpy as np

    out = dict(_drawn_inputs(seed))
    spreads = {'L3_gnn_b1': (0.0, 0.8),
     'L3_gnn_b2': (0.0, 0.1),
     'L3_gnn_bd1': (0.0, 0.289),
     'L3_gnn_bd2': (0.0, 0.1)}
    factors = {'L1_gnn_b_ir': 4.216,
     'L1_gnn_W_hr': 8.0,
     'L1_gnn_b_hr': 64.0,
     'L1_gnn_W_xr': 7.006,
     'L1_gnn_b_xr': 64.0,
     'L1_gnn_b_hz': 8.0,
     'L1_gnn_b_xz': 8.0,
     'L1_gnn_b_hm': 7.187,
     'L1_gnn_b_xm': 3.334,
     'L3_gnn_W1': 8.0,
     'L3_gnn_W2': 4.846,
     'L1_gnn_W_ir': 2.805}
    for name, (base, spread) in spreads.items():
        noise = np.random.default_rng([zlib.crc32(name.encode()), seed]).standard_normal(out[name].shape)
        drawn = base * np.exp(spread * noise) if base else spread * noise
        out[name] = jnp.asarray(drawn.astype(out[name].dtype))
    for name, factor in factors.items():
        out[name] = (out[name] * factor).astype(out[name].dtype)
    return out
```

```python
from contextlib import ExitStack

import numpy as np

import concourse.bass as bass
from concourse import mybir

ALU = mybir.AluOpType
ACT = mybir.ActivationFunctionType
AX_X = mybir.AxisListType.X
F32 = mybir.dt.float32
BF16 = mybir.dt.bfloat16

P = 128
NG = 64
CUTOFF = 5.0
LN2 = float(np.log(2.0))
LN_EPS = 1e-5
DEG_EPS = 1e-6
EXP_CAP = 2.0 ** 60

(W0T, WIR, WIZ, WIM, WXR, WXZ, WXM, WHR, WHZ, WHM, THETA, WAT, W2T, WD1T, WD2T, IDENT, OFFD) = range(17)
(C_XR, C_HR, C_XZ, C_HZ, C_XM, C_HM, C_B1, C_B2, C_BD1, C_NOFF) = range(10)
(R_B0, R_IR, R_IZ, R_IM, R_BIAS2, R_BD2) = range(6)

ROWS = 8
HALF = ROWS // 2
GPB = P // ROWS
YRING = 4


def is_later(k, d):
    return k >= d if isinstance(k, int) else True


def run_steps(eng, total, lags, body):
    for k in range(min(4, total)):
        body(k, k % 2, lambda lag: k - lag >= 0)
    if total > 4:
        with eng.Fori(2, total // 2) as i:
            for u in range(2):
                body(2 * i + u, u, lambda lag: True)
    for k in range(total, total + lags):
        body(k, k % 2, lambda lag: 0 <= k - lag < total)


def build(nc, B, x, adj, adjt, weights, w1t, columns, rows, halves, out, parts):
    offsets = np.linspace(0.0, CUTOFF, NG, dtype=np.float32)
    width = offsets[1] - offsets[0]
    coeff = float(np.float32(-0.5) / (width * width))

    ctx = ExitStack()
    with ctx:
        def sb(name, shape, dt=F32):
            return ctx.enter_context(nc.sbuf_tensor(name, shape, dt))

        def sem(name):
            return ctx.enter_context(nc.semaphore(name))

        x_all = sb("x_all", [P, B * P])
        adj_t = sb("adj_t", [P, B * P])
        big = sb("big", [P, 3 * B * P])
        wt = sb("wt", [P, 17, P])
        w1 = sb("w1", [P, P])
        col = sb("col", [P, 10])
        row = sb("row", [P, 6, P])
        half_f = sb("half_f", [6, P])
        half = sb("half", [6, P], BF16)
        b_gate = sb("b_gate", [P, 2])
        b1_ln2 = sb("b1_ln2", [P, 1])
        bd1_ln2 = sb("bd1_ln2", [P, 1])
        deg = sb("deg", [P, 2, B])
        root = sb("root", [P, 2, B])
        dinv = sb("dinv", [P, 2, B])
        mean = sb("mean", [P, B])
        part_sq = sb("part_sq", [P, 2, B])
        var_eps = sb("var_eps", [P, B])
        std = sb("std", [P, B])
        rstd = sb("rstd", [P, B])
        six = sb("six", [P, B, 6])

        ident = wt[:, IDENT, :]

        def at(t, b):
            return t[:, b * P:(b + 1) * P] if isinstance(b, int) else t[:, bass.ds(b * P, P)]

        def column(t, b):
            return t[:, b:b + 1] if isinstance(b, int) else t[:, bass.ds(b, 1)]

        CH = min(8, B)
        with ExitStack() as cx, nc.Block() as block:
            s_w, s_x, s_at, s_an = (cx.enter_context(nc.semaphore(n)) for n in ("ld_w", "ld_x", "ld_adj_t", "ld_adj"))
            deg_sum = cx.enter_context(nc.semaphore("deg_sum"))
            deg_sh = cx.enter_context(nc.semaphore("deg_shifted"))
            root_ok = cx.enter_context(nc.semaphore("root_ok"))
            adj_n = big[:, 0:B * P]

            @block.sync
            def _(sp):
                sp.dma_start(adj_n.rearrange("p (b j) -> p b j", j=P), adj.rearrange("b i j -> i b j")).then_inc(s_an, 16)
                sp.dma_start(x_all[:, :].rearrange("p (b j) -> p b j", j=P), x.rearrange("b i j -> i b j")).then_inc(s_x, 16)
                sp.dma_start(adj_t[:, :].rearrange("p (b j) -> p b j", j=P), adjt.rearrange("b i j -> i b j")).then_inc(s_at, 16)
                sp.wait_ge(s_an, 16)
                sp.wait_ge(s_x, 16)
                sp.wait_ge(s_at, 16)

            @block.scalar
            def _(act):
                act.dma_start(wt[:, :, :], weights).then_inc(s_w, 16)
                act.dma_start(w1[0:NG, :], w1t).then_inc(s_w, 16)
                act.dma_start(w1[NG:P, :], w1t).then_inc(s_w, 16)
                act.dma_start(col[:, :], columns).then_inc(s_w, 16)
                act.dma_start(row[:, :, :], rows.partition_broadcast(P)).then_inc(s_w, 16)
                act.dma_start(half_f[:, :], halves).then_inc(s_w, 16)
                act.wait_ge(deg_sh, 2)
                nc.scalar.activation(root[:, :, :], deg[:, :, :], ACT.Sqrt).then_inc(root_ok, 1)

            @block.vector
            def _(dve):
                dve.wait_ge(s_an, 16)
                nc.vector.tensor_reduce(deg[:, 0, :], adj_n.rearrange("p (b j) -> p b j", j=P), axis=AX_X, op=ALU.add).then_inc(deg_sum, 1)
                dve.wait_ge(deg_sum, 1)
                nc.vector.tensor_scalar_add(deg[:, 1, :], deg[:, 0, :], 1.0).then_inc(deg_sh, 1)
                dve.wait_ge(deg_sh, 1)
                nc.vector.tensor_scalar_add(deg[:, 0, :], deg[:, 1, :], DEG_EPS).then_inc(deg_sh, 1)
                dve.wait_ge(s_w, 96)
                nc.vector.tensor_copy(half[:, :], half_f[:, :])
                nc.vector.tensor_tensor(b_gate[:, 0:1], col[:, C_XR:C_XR + 1], col[:, C_HR:C_HR + 1], ALU.add)
                nc.vector.tensor_tensor(b_gate[:, 1:2], col[:, C_XZ:C_XZ + 1], col[:, C_HZ:C_HZ + 1], ALU.add)
                nc.vector.tensor_scalar_add(b1_ln2[:, :], col[:, C_B1:C_B1 + 1], -LN2)
                nc.vector.tensor_scalar_add(bd1_ln2[:, :], col[:, C_BD1:C_BD1 + 1], -LN2)
                dve.wait_ge(root_ok, 1)
                nc.vector.reciprocal(dinv[:, :, :], root[:, :, :])

        def rstd_phase(name):
            with ExitStack() as cx, nc.Block() as block:
                step = cx.enter_context(nc.semaphore(name + "_step"))
                ve_ok = cx.enter_context(nc.semaphore(name + "_var_eps"))
                std_ok = cx.enter_context(nc.semaphore(name + "_std"))

                @block.vector
                def _(dve):
                    nc.vector.tensor_tensor(mean[:, :], six[:, :, 1], six[:, :, 4], ALU.add).then_inc(step, 1)
                    nc.vector.tensor_tensor(part_sq[:, 0, :], six[:, :, 1], six[:, :, 4], ALU.subtract).then_inc(step, 1)
                    nc.vector.tensor_tensor(var_eps[:, :], six[:, :, 2], six[:, :, 5], ALU.add).then_inc(step, 1)
                    dve.wait_ge(step, 3)
                    nc.vector.tensor_scalar(mean[:, :], mean[:, :], 0.5, None, ALU.mult)
                    nc.vector.tensor_tensor(part_sq[:, 1, :], part_sq[:, 0, :], part_sq[:, 0, :], ALU.mult).then_inc(step, 1)
                    nc.vector.tensor_scalar(var_eps[:, :], var_eps[:, :], 1.0 / P, LN_EPS, ALU.mult, ALU.add).then_inc(step, 1)
                    dve.wait_ge(step, 5)
                    nc.vector.scalar_tensor_tensor(var_eps[:, :], part_sq[:, 1, :], 0.25, var_eps[:, :], ALU.mult, ALU.add).then_inc(ve_ok, 1)
                    dve.wait_ge(std_ok, 1)
                    nc.vector.reciprocal(rstd[:, :], std[:, :])

                @block.scalar
                def _(act):
                    act.wait_ge(ve_ok, 1)
                    nc.scalar.activation(std[:, :], var_eps[:, :], ACT.Sqrt).then_inc(std_ok, 1)

        def normalise(dst, src, b):
            return nc.vector.tensor_scalar(dst, src, column(mean, b),
                                           column(rstd, b), ALU.subtract, ALU.mult)

        def row_stats(b):
            dst = six[:, b, :] if isinstance(b, int) else six[:, bass.ds(b, 1), :].rearrange("p a c -> p (a c)")
            nc.vector.bn_stats(dst, at(x_all, b))

        with ExitStack() as cx, nc.Block() as block:
            def tmp(name, shape, dt=F32):
                return cx.enter_context(nc.sbuf_tensor("l0_" + name, shape, dt))

            def ps(name):
                return cx.enter_context(nc.psum_tensor("l0_" + name, [P, 2, 512], F32))

            ah, xs, st, t_o = (tmp(n, [P, 2, P]) for n in ("ah", "xs", "st", "t"))
            ps_s, ps_o = ps("ps_s"), ps("ps_o")
            ah_ok, xs_ok, s_ok, st_ok, o_ok, t_ok, r_ok = (
                cx.enter_context(nc.semaphore("l0_" + n))
                for n in ("ah_ok", "xs_ok", "s_ok", "st_ok", "o_ok", "t_ok", "r_ok"))

            @block.gpsimd
            def _(pool):
                def body(b, u, live):
                    if is_later(b, 2):
                        pool.wait_ge(s_ok, b - 1)
                    nc.gpsimd.tensor_tensor(ah[:, u, :], at(adj_t, b), ident, ALU.add).then_inc(ah_ok, 1)
                run_steps(pool, B, 0, body)

            @block.tensor
            def _(pe):
                def body(b, u, live):
                    if live(0):
                        pe.wait_ge(ah_ok, b + 1)
                        pe.wait_ge(xs_ok, b + 1)
                        if is_later(b, 2):
                            pe.wait_ge(st_ok, b - 1)
                        nc.tensor.matmul(ps_s[:, u, 0:P], xs[:, u, :], ah[:, u, :], start=True, stop=True).then_inc(s_ok, 1)
                    if live(1):
                        c, v = b - 1, 1 - u
                        pe.wait_ge(st_ok, c + 1)
                        if is_later(c, 2):
                            pe.wait_ge(t_ok, c - 1)
                        nc.tensor.matmul(ps_o[:, v, 0:P], st[:, v, :], wt[:, W0T, :], start=True, stop=True).then_inc(o_ok, 1)
                run_steps(pe, B, 1, body)

            @block.scalar
            def _(act):
                def body(b, u, live):
                    act.wait_ge(s_ok, b + 1)
                    if is_later(b, 2):
                        act.wait_ge(o_ok, b - 1)
                    nc.scalar.copy(st[:, u, :], ps_s[:, u, 0:P]).then_inc(st_ok, 1)
                run_steps(act, B, 0, body)

            @block.vector
            def _(dve):
                def body(b, u, live):
                    if live(0):
                        if is_later(b, 2):
                            dve.wait_ge(s_ok, b - 1)
                        nc.vector.tensor_scalar(xs[:, u, :], at(x_all, b), column(dinv[:, 0, :], b), None, ALU.mult).then_inc(xs_ok, 1)
                    if live(2):
                        dve.wait_ge(r_ok, b - 1)
                    if live(1):
                        c, v = b - 1, 1 - u
                        dve.wait_ge(o_ok, c + 1)
                        nc.vector.scalar_tensor_tensor(t_o[:, v, :], ps_o[:, v, 0:P], column(dinv[:, 0, :], c), row[:, R_B0, :],
                                                       ALU.mult, ALU.add).then_inc(t_ok, 1)
                    if live(2):
                        row_stats(b - 2)
                    if live(1):
                        dve.wait_ge(t_ok, c + 1)
                        nc.vector.scalar_tensor_tensor(at(x_all, c), t_o[:, v, :], 0.0, at(x_all, c), ALU.max, ALU.add).then_inc(r_ok, 1)
                run_steps(dve, B, 2, body)

        rstd_phase("ln0")

        gates = big[:, :].rearrange("p (t c b) -> p t c b", c=3, b=B)
        with ExitStack() as cx, nc.Block() as block:
            def tmp(name, shape, dt=F32):
                return cx.enter_context(nc.sbuf_tensor("l1_" + name, shape, dt))

            def ps(name):
                return cx.enter_context(nc.psum_tensor("l1_" + name, [P, 2, 512], F32))

            x1, x1t, gt = (tmp(n, [P, 2, P]) for n in ("x1", "x1t", "gt"))
            proj = tmp("proj", [P, 2, 3 * P])
            ps_t, ps_p, ps_a = ps("ps_t"), ps("ps_p"), ps("ps_a")
            n_ok, cp_ok, g_ok, t_ok, xt_ok, p_ok, pj_ok, a_ok, ev_ok = (
                cx.enter_context(nc.semaphore("l1_" + n))
                for n in ("n_ok", "cp_ok", "g_ok", "t_ok", "xt_ok", "p_ok", "pj_ok", "a_ok", "ev_ok"))

            @block.gpsimd
            def _(pool):
                def body(b, u, live):
                    if is_later(b, 2):
                        pool.wait_ge(a_ok, b - 1)
                    pool.wait_ge(n_ok, b + 1)
                    nc.gpsimd.tensor_tensor(gt[:, u, :], at(adj_t, b), wt[:, OFFD, :], ALU.mult).then_inc(g_ok, 1)
                    nc.gpsimd.tensor_copy(at(x_all, b), x1[:, u, :]).then_inc(cp_ok, 1)
                run_steps(pool, B, 0, body)

            @block.vector
            def _(dve):
                def body(b, u, live):
                    if live(0):
                        if is_later(b, 2):
                            dve.wait_ge(t_ok, b - 1)
                            dve.wait_ge(cp_ok, b - 1)
                        normalise(x1[:, u, :], at(x_all, b), b).then_inc(n_ok, 1)
                    if live(1):
                        c, v = b - 1, 1 - u
                        dve.wait_ge(p_ok, c + 1)
                        if is_later(c, 2):
                            dve.wait_ge(a_ok, c - 1)
                        nc.vector.tensor_tensor(proj[:, v, :], ps_p[:, v, 0:3 * P],
                                                row[:, R_IR:R_IM + 1, :].rearrange("p a b -> p (a b)"), ALU.add).then_inc(pj_ok, 1)
                run_steps(dve, B, 1, body)

            @block.tensor
            def _(pe):
                def body(b, u, live):
                    if live(0):
                        pe.wait_ge(n_ok, b + 1)
                        if is_later(b, 2):
                            pe.wait_ge(xt_ok, b - 1)
                        nc.tensor.transpose(ps_t[:, u, 0:P], x1[:, u, :], ident).then_inc(t_ok, 1)
                    if live(2):
                        c = b - 2
                        pe.wait_ge(pj_ok, c + 1)
                        pe.wait_ge(g_ok, c + 1)
                        if is_later(c, 2):
                            pe.wait_ge(ev_ok, 3 * (c - 1))
                        for a in range(3):
                            nc.tensor.matmul(ps_a[:, u, a * P:(a + 1) * P], wt[:, WXR + a, :], x1t[:, u, :], start=True, stop=False)
                            last = nc.tensor.matmul(ps_a[:, u, a * P:(a + 1) * P], proj[:, u, a * P:(a + 1) * P], gt[:, u, :],
                                                    start=False, stop=True)
                        last.then_inc(a_ok, 1)
                    if live(1):
                        c, v = b - 1, 1 - u
                        pe.wait_ge(xt_ok, c + 1)
                        if is_later(c, 2):
                            pe.wait_ge(pj_ok, c - 1)
                        nc.tensor.matmul(ps_p[:, v, 0:3 * P], x1t[:, v, :], wt[:, WIR:WIM + 1, :].rearrange("p a b -> p (a b)"),
                                         start=True, stop=True).then_inc(p_ok, 1)
                run_steps(pe, B, 2, body)

            @block.scalar
            def _(act):
                def body(b, u, live):
                    if live(2):
                        c = b - 2
                        act.wait_ge(a_ok, c + 1)
                        for a, bias in enumerate((b_gate[:, 0:1], b_gate[:, 1:2], col[:, C_XM:C_XM + 1])):
                            dst = gates[:, :, a, c] if isinstance(c, int) else gates[:, :, a, bass.ds(c, 1)].rearrange("p t o -> p (t o)")
                            nc.scalar.activation(dst, ps_a[:, u, a * P:(a + 1) * P], ACT.Identity, bias=bias).then_inc(ev_ok, 1)
                    if live(0):
                        act.wait_ge(t_ok, b + 1)
                        if is_later(b, 2):
                            act.wait_ge(a_ok, b - 1)
                        nc.scalar.copy(x1t[:, u, :], ps_t[:, u, 0:P]).then_inc(xt_ok, 1)
                run_steps(act, B, 2, body)

        with ExitStack() as cx, nc.Block() as block:
            def tmp(name, shape, dt=F32):
                return cx.enter_context(nc.sbuf_tensor("gru_" + name, shape, dt))

            def ps(name):
                return cx.enter_context(nc.psum_tensor("gru_" + name, [P, 2, 512], F32))

            r, z, m, t1, t2, omz, zh, om = (tmp(n, [P, 2, B]) for n in ("r", "z", "m", "t1", "t2", "omz", "zh", "om"))
            zero = tmp("zero", [P, B])
            CUT = 2
            an = tmp("an", [P, 2, CUT * P])
            rest = tmp("rest", [P, 2, CUT * P])
            cut = tmp("cut", [P, 2, 3, CUT * P], BF16)
            ps_r, ps_z, ps_m = ps("ps_r"), ps("ps_z"), ps("ps_m")
            (init_ok, r_mm, m_mm, z_mm, r_s, z_s, m_s, t1_ok, t2_ok, zh_ok, omz_ok, om_ok, h_ok) = (
                cx.enter_context(nc.semaphore("gru_" + n))
                for n in ("init", "r_mm", "m_mm", "z_mm", "r_s", "z_s", "m_s", "t1_ok", "t2_ok", "zh_ok", "omz_ok", "om_ok", "h_ok"))
            an_in = [cx.enter_context(nc.semaphore(f"cut_in{u}")) for u in range(2)]
            cut_out = [cx.enter_context(nc.semaphore(f"cut_out{u}")) for u in range(2)]
            cut_step = cx.enter_context(nc.semaphore("cut_step"))

            @block.vector
            def _(dve):
                nc.vector.memset(zero[:, :], 0.0).then_inc(init_ok, 1)
                nc.vector.memset(zh[:, 1, :], 0.0).then_inc(init_ok, 1)
                nc.vector.memset(om[:, 1, :], 0.0).then_inc(init_ok, 1)
                dve.wait_ge(init_ok, 3)

                def body(t, u, live):
                    g = gates[:, t, :, :] if isinstance(t, int) else gates[:, bass.ds(t, 1), :, :].rearrange("p o c b -> p (o c) b")
                    if isinstance(t, int):
                        before = zero[:, :] if t == 0 else gates[:, t - 1, 0, :]
                    else:
                        before = gates[:, bass.ds(t - 1, 1), 0, :].rearrange("p o b -> p (o b)")
                    dve.wait_ge(m_mm, t + 1)
                    dve.wait_ge(r_s, t + 1)
                    nc.vector.scalar_tensor_tensor(t1[:, u, :], ps_m[:, u, 0:B], col[:, C_HM:C_HM + 1], r[:, u, :],
                                                   ALU.add, ALU.mult).then_inc(t1_ok, 1)
                    dve.wait_ge(t1_ok, t + 1)
                    nc.vector.tensor_tensor(t2[:, u, :], t1[:, u, :], g[:, 2, :], ALU.add).then_inc(t2_ok, 1)
                    dve.wait_ge(z_s, t + 1)
                    if is_later(t, 1):
                        dve.wait_ge(h_ok, t)
                    nc.vector.tensor_tensor(zh[:, u, :], z[:, u, :], before, ALU.mult).then_inc(zh_ok, 1)
                    nc.vector.tensor_scalar(omz[:, u, :], z[:, u, :], -1.0, 1.0, ALU.mult, ALU.add).then_inc(omz_ok, 1)
                    dve.wait_ge(omz_ok, t + 1)
                    dve.wait_ge(m_s, t + 1)
                    nc.vector.tensor_tensor(om[:, u, :], omz[:, u, :], m[:, u, :], ALU.mult).then_inc(om_ok, 1)
                    dve.wait_ge(zh_ok, t + 1)
                    dve.wait_ge(om_ok, t + 1)
                    nc.vector.tensor_tensor(g[:, 0, :], om[:, u, :], zh[:, u, :], ALU.add).then_inc(h_ok, 1)
                run_steps(dve, P, 0, body)

            @block.scalar
            def _(act):
                def body(t, u, live):
                    act.wait_ge(r_mm, t + 1)
                    nc.scalar.activation(r[:, u, :], ps_r[:, u, 0:B], ACT.Sigmoid).then_inc(r_s, 1)
                    act.wait_ge(z_mm, t + 1)
                    nc.scalar.activation(z[:, u, :], ps_z[:, u, 0:B], ACT.Sigmoid).then_inc(z_s, 1)
                    act.wait_ge(t2_ok, t + 1)
                    nc.scalar.activation(m[:, u, :], t2[:, u, :], ACT.Tanh).then_inc(m_s, 1)
                nc.scalar.preload_act_table_set("sigmoid_and_others")
                run_steps(act, P, 0, body)

            @block.tensor
            def _(pe):
                def seed(t, u):
                    for c, dst in enumerate((ps_r, ps_z)):
                        src = gates[:, t, c, :] if isinstance(t, int) else gates[:, bass.ds(t, 1), c, :].rearrange("p o b -> p (o b)")
                        nc.tensor.matmul(dst[:, u, 0:B], ident, src, start=True, stop=False)

                seed(0, 0)
                pe.wait_ge(init_ok, 3)

                def body(t, u, live):
                    v = 1 - u
                    if is_later(t, 1):
                        pe.wait_ge(zh_ok, t)
                    nc.tensor.matmul(ps_r[:, u, 0:B], wt[:, WHR, :], zh[:, v, :], start=False, stop=False)
                    nc.tensor.matmul(ps_m[:, u, 0:B], wt[:, WHM, :], zh[:, v, :], start=True, stop=False)
                    nc.tensor.matmul(ps_z[:, u, 0:B], wt[:, WHZ, :], zh[:, v, :], start=False, stop=False)
                    if is_later(t, 1):
                        pe.wait_ge(om_ok, t)
                    nc.tensor.matmul(ps_r[:, u, 0:B], wt[:, WHR, :], om[:, v, :], start=False, stop=True).then_inc(r_mm, 1)
                    nc.tensor.matmul(ps_m[:, u, 0:B], wt[:, WHM, :], om[:, v, :], start=False, stop=True).then_inc(m_mm, 1)
                    nc.tensor.matmul(ps_z[:, u, 0:B], wt[:, WHZ, :], om[:, v, :], start=False, stop=True).then_inc(z_mm, 1)
                    if not (isinstance(t, int) and t == P - 1):
                        seed(t + 1, v)
                for t in range(4):
                    body(t, t % 2, None)
                with pe.Fori(2, P // 2 - 1) as i:
                    for u in range(2):
                        body(2 * i + u, u, None)
                for t in range(P - 2, P):
                    body(t, t % 2, None)

            @block.sync
            def _(sp):
                for c in range(B // CUT + 1):
                    if c < B // CUT:
                        if c >= 2:
                            sp.wait_ge(cut_step, 5 * (c - 1))
                        sp.dma_start(an[:, c % 2, :].rearrange("i (b j) -> i b j", j=P),
                                     adj[c * CUT:(c + 1) * CUT].rearrange("b i j -> i b j")).then_inc(an_in[c % 2], 16)
                    if c >= 1:
                        sp.wait_ge(cut_step, 5 * c)
                        for part in range(3):
                            sp.dma_start(parts[part, (c - 1) * CUT:c * CUT].rearrange("b i j -> i b j"),
                                         cut[:, (c - 1) % 2, part, :].rearrange("i (b j) -> i b j", j=P)).then_inc(cut_out[(c - 1) % 2], 16)
                for u in range(2):
                    sp.wait_ge(cut_out[u], 48 * ((B // CUT + 1 - u) // 2))

            @block.gpsimd
            def _(pool):
                for c in range(B // CUT):
                    u = c % 2
                    pool.wait_ge(an_in[u], 16 * (c // 2 + 1))
                    if c >= 2:
                        pool.wait_ge(cut_out[u], 48 * (c // 2))
                    nc.gpsimd.tensor_copy(cut[:, u, 0, :], an[:, u, :]).then_inc(cut_step, 1)
                    pool.wait_ge(cut_step, 5 * c + 1)
                    nc.gpsimd.tensor_tensor(rest[:, u, :], an[:, u, :], cut[:, u, 0, :], ALU.subtract).then_inc(cut_step, 1)
                    pool.wait_ge(cut_step, 5 * c + 2)
                    nc.gpsimd.tensor_copy(cut[:, u, 1, :], rest[:, u, :]).then_inc(cut_step, 1)
                    pool.wait_ge(cut_step, 5 * c + 3)
                    nc.gpsimd.tensor_tensor(an[:, u, :], rest[:, u, :], cut[:, u, 1, :], ALU.subtract).then_inc(cut_step, 1)
                    pool.wait_ge(cut_step, 5 * c + 4)
                    nc.gpsimd.tensor_copy(cut[:, u, 2, :], an[:, u, :]).then_inc(cut_step, 1)

        with ExitStack() as cx, nc.Block() as block:
            hs = cx.enter_context(nc.sbuf_tensor("l1_hs", [P, 2, P], F32))
            ps_t = cx.enter_context(nc.psum_tensor("l1_ps_h", [P, 2, 512], F32))
            h_ok, t_ok, r_ok = (cx.enter_context(nc.semaphore("l1s_" + n)) for n in ("h_ok", "t_ok", "r_ok"))

            @block.scalar
            def _(act):
                def body(b, u, live):
                    if is_later(b, 2):
                        act.wait_ge(t_ok, b - 1)
                    src = gates[:, :, 0, b] if isinstance(b, int) else gates[:, :, 0, bass.ds(b, 1)].rearrange("p t o -> p (t o)")
                    nc.scalar.activation(hs[:, u, :], src, ACT.Relu).then_inc(h_ok, 1)
                run_steps(act, B, 0, body)

            @block.tensor
            def _(pe):
                def body(b, u, live):
                    pe.wait_ge(h_ok, b + 1)
                    if is_later(b, 2):
                        pe.wait_ge(r_ok, b - 1)
                    nc.tensor.transpose(ps_t[:, u, 0:P], hs[:, u, :], ident).then_inc(t_ok, 1)
                run_steps(pe, B, 0, body)

            @block.vector
            def _(dve):
                def body(b, u, live):
                    if live(1):
                        dve.wait_ge(r_ok, b)
                    if live(0):
                        dve.wait_ge(t_ok, b + 1)
                        nc.vector.tensor_tensor(at(x_all, b), ps_t[:, u, 0:P], at(x_all, b), ALU.add).then_inc(r_ok, 1)
                    if live(1):
                        row_stats(b - 1)
                run_steps(dve, B, 1, body)

        rstd_phase("ln1")

        with ExitStack() as cx, nc.Block() as block:
            def tmp(name, shape, dt=F32):
                return cx.enter_context(nc.sbuf_tensor("l2_" + name, shape, dt))

            def ps(name):
                return cx.enter_context(nc.psum_tensor("l2_" + name, [P, 2, 512], F32))

            x2, x2t, ah, sup, t_o = (tmp(n, [P, 2, P]) for n in ("x2", "x2t", "ah", "sup", "t"))
            ps_t, ps_u, ps_o = ps("ps_t"), ps("ps_u"), ps("ps_o")
            n_ok, cp_ok, ah_ok, t_ok, xt_ok, u_ok, sup_ok, o_ok, to_ok, r_ok = (
                cx.enter_context(nc.semaphore("l2_" + n))
                for n in ("n_ok", "cp_ok", "ah_ok", "t_ok", "xt_ok", "u_ok", "sup_ok", "o_ok", "to_ok", "r_ok"))

            @block.gpsimd
            def _(pool):
                def body(b, u, live):
                    if is_later(b, 2):
                        pool.wait_ge(o_ok, b - 1)
                    pool.wait_ge(n_ok, b + 1)
                    nc.gpsimd.tensor_tensor(ah[:, u, :], at(adj_t, b), ident, ALU.add).then_inc(ah_ok, 1)
                    nc.gpsimd.tensor_copy(at(x_all, b), x2[:, u, :]).then_inc(cp_ok, 1)
                run_steps(pool, B, 0, body)

            @block.tensor
            def _(pe):
                def body(b, u, live):
                    if live(0):
                        pe.wait_ge(n_ok, b + 1)
                        if is_later(b, 2):
                            pe.wait_ge(xt_ok, b - 1)
                        nc.tensor.transpose(ps_t[:, u, 0:P], x2[:, u, :], ident).then_inc(t_ok, 1)
                    if live(2):
                        c = b - 2
                        pe.wait_ge(sup_ok, c + 1)
                        pe.wait_ge(ah_ok, c + 1)
                        if is_later(c, 2):
                            pe.wait_ge(to_ok, c - 1)
                        nc.tensor.matmul(ps_o[:, u, 0:P], ah[:, u, :], sup[:, u, :], start=True, stop=True).then_inc(o_ok, 1)
                    if live(1):
                        c, v = b - 1, 1 - u
                        pe.wait_ge(xt_ok, c + 1)
                        if is_later(c, 2):
                            pe.wait_ge(sup_ok, c - 1)
                        nc.tensor.matmul(ps_u[:, v, 0:P], x2t[:, v, :], wt[:, THETA, :], start=True, stop=True).then_inc(u_ok, 1)
                run_steps(pe, B, 2, body)

            @block.scalar
            def _(act):
                def body(b, u, live):
                    if live(0):
                        act.wait_ge(t_ok, b + 1)
                        if is_later(b, 2):
                            act.wait_ge(u_ok, b - 1)
                        nc.scalar.copy(x2t[:, u, :], ps_t[:, u, 0:P]).then_inc(xt_ok, 1)
                    if live(1):
                        c, v = b - 1, 1 - u
                        act.wait_ge(u_ok, c + 1)
                        if is_later(c, 2):
                            act.wait_ge(o_ok, c - 1)
                        nc.scalar.activation(sup[:, v, :], ps_u[:, v, 0:P], ACT.Copy, scale=column(dinv[:, 1, :], c)).then_inc(sup_ok, 1)
                run_steps(act, B, 1, body)

            @block.vector
            def _(dve):
                def body(b, u, live):
                    if live(0):
                        if is_later(b, 2):
                            dve.wait_ge(t_ok, b - 1)
                            dve.wait_ge(cp_ok, b - 1)
                        normalise(x2[:, u, :], at(x_all, b), b).then_inc(n_ok, 1)
                    if live(3):
                        dve.wait_ge(r_ok, b - 2)
                    if live(2):
                        c = b - 2
                        dve.wait_ge(o_ok, c + 1)
                        nc.vector.scalar_tensor_tensor(t_o[:, u, :], ps_o[:, u, 0:P], column(dinv[:, 1, :], c), row[:, R_BIAS2, :],
                                                       ALU.mult, ALU.add).then_inc(to_ok, 1)
                    if live(3):
                        row_stats(b - 3)
                    if live(2):
                        dve.wait_ge(to_ok, c + 1)
                        dve.wait_ge(cp_ok, c + 1)
                        nc.vector.tensor_tensor(at(x_all, c), t_o[:, u, :], at(x_all, c), ALU.add).then_inc(r_ok, 1)
                run_steps(dve, B, 3, body)

        rstd_phase("ln2")

        rf_all = big[:, 0:B * P]
        y_all = big[:, B * P:2 * B * P]
        with ExitStack() as cx, nc.Block() as block:
            def tmp(name, shape, dt=F32):
                return cx.enter_context(nc.sbuf_tensor("l3p_" + name, shape, dt))

            def ps(name):
                return cx.enter_context(nc.psum_tensor("l3p_" + name, [P, 2, 512], F32))

            x3, x3t, rfs = (tmp(n, [P, 2, P]) for n in ("x3", "x3t", "rfs"))
            ps_t, ps_f, ps_q = ps("ps_t"), ps("ps_f"), ps("ps_q")
            n_ok, cp_ok, sq_ok, t_ok, xt_ok, f_ok, rfs_ok, rf_ok, q_ok, y_ok = (
                cx.enter_context(nc.semaphore("l3p_" + n))
                for n in ("n_ok", "cp_ok", "sq_ok", "t_ok", "xt_ok", "f_ok", "rfs_ok", "rf_ok", "q_ok", "y_ok"))

            @block.gpsimd
            def _(pool):
                def body(b, u, live):
                    pool.wait_ge(n_ok, b + 1)
                    nc.gpsimd.tensor_tensor(at(adj_t, b), at(adj_t, b), at(adj_t, b), ALU.mult).then_inc(sq_ok, 1)
                    nc.gpsimd.tensor_copy(at(x_all, b), x3[:, u, :]).then_inc(cp_ok, 1)
                run_steps(pool, B, 0, body)

            @block.tensor
            def _(pe):
                def body(b, u, live):
                    if live(0):
                        pe.wait_ge(n_ok, b + 1)
                        if is_later(b, 2):
                            pe.wait_ge(xt_ok, b - 1)
                        nc.tensor.transpose(ps_t[:, u, 0:P], x3[:, u, :], ident).then_inc(t_ok, 1)
                    if live(2):
                        c = b - 2
                        pe.wait_ge(rfs_ok, c + 1)
                        pe.wait_ge(sq_ok, c + 1)
                        if is_later(c, 2):
                            pe.wait_ge(y_ok, c - 1)
                        nc.tensor.matmul(ps_q[:, u, 0:P], rfs[:, u, :], at(adj_t, c), start=True, stop=True).then_inc(q_ok, 1)
                    if live(1):
                        c, v = b - 1, 1 - u
                        pe.wait_ge(xt_ok, c + 1)
                        if is_later(c, 2):
                            pe.wait_ge(rfs_ok, c - 1)
                        nc.tensor.matmul(ps_f[:, v, 0:P], x3t[:, v, :], wt[:, WAT, :], start=True, stop=True).then_inc(f_ok, 1)
                run_steps(pe, B, 2, body)

            @block.scalar
            def _(act):
                def body(b, u, live):
                    if live(0):
                        act.wait_ge(t_ok, b + 1)
                        if is_later(b, 2):
                            act.wait_ge(f_ok, b - 1)
                        nc.scalar.copy(x3t[:, u, :], ps_t[:, u, 0:P]).then_inc(xt_ok, 1)
                    if live(1):
                        c, v = b - 1, 1 - u
                        act.wait_ge(f_ok, c + 1)
                        if is_later(c, 2):
                            act.wait_ge(q_ok, c - 1)
                            act.wait_ge(rf_ok, c - 1)
                        nc.scalar.copy(rfs[:, v, :], ps_f[:, v, 0:P]).then_inc(rfs_ok, 1)
                run_steps(act, B, 1, body)

            @block.vector
            def _(dve):
                def body(b, u, live):
                    if live(0):
                        if is_later(b, 2):
                            dve.wait_ge(t_ok, b - 1)
                            dve.wait_ge(cp_ok, b - 1)
                        normalise(x3[:, u, :], at(x_all, b), b).then_inc(n_ok, 1)
                    if live(1):
                        c, v = b - 1, 1 - u
                        dve.wait_ge(rfs_ok, c + 1)
                        nc.vector.tensor_copy(at(rf_all, c), rfs[:, v, :]).then_inc(rf_ok, 1)
                    if live(2):
                        c = b - 2
                        dve.wait_ge(q_ok, c + 1)
                        nc.vector.tensor_scalar(at(y_all, c), ps_q[:, u, 0:P], col[:, C_B2:C_B2 + 1], None, ALU.mult).then_inc(y_ok, 1)
                run_steps(dve, B, 2, body)

        e_ring = big[:, 2 * B * P:3 * B * P].bitcast(BF16)
        e_ring = e_ring[0:6, 0:2 * GPB * 512] if B * P * 2 >= 2 * GPB * 512 else None
        K = B * GPB
        with ExitStack() as cx, nc.Block() as block:
            def tmp(name, shape, dt=F32):
                return cx.enter_context(nc.sbuf_tensor("l3_" + name, shape, dt))

            if e_ring is None:
                e_ring = tmp("e_ring", [6, 2 * GPB * 512], BF16)[:, :]
            dist2 = tmp("dist2", [P, 512])
            gauss = tmp("gauss", [P, 2, 512])
            ex = tmp("ex", [P, 2, 1024])
            h = tmp("h", [P, 2, 1024])
            zt = tmp("zt", [P, 2, 1024])
            ps_e = cx.enter_context(nc.psum_tensor("l3_ps_e", [P, 512], F32))
            ps_v = cx.enter_context(nc.psum_tensor("l3_ps_v", [P, 2, 1024], F32))
            ps_w = cx.enter_context(nc.psum_tensor("l3_ps_w", [P, 2, 512], F32))
            ps_y = cx.enter_context(nc.psum_tensor("l3_ps_y", [P, 512], F32))
            (e_mm, sq_ok, g_ok, v_mm, ev_ok, cap_ok, ln_ok, h_ok, w_mm, z_ok, y_mm, y_ev) = (
                cx.enter_context(nc.semaphore("l3_" + n))
                for n in ("e_mm", "sq_ok", "g_ok", "v_mm", "ev_ok", "cap_ok", "ln_ok", "h_ok", "w_mm", "z_ok", "y_mm", "y_ev"))
            e_in = [cx.enter_context(nc.semaphore(f"l3_e_in{u}")) for u in range(2)]

            def cols(t, start, n):
                return t[:, start:start + n] if isinstance(start, int) else t[:, bass.ds(start, n)]

            def all_groups(eng, lags, body, at_graph=None):
                for k in range(4):
                    body(k, k % 2, lambda lag: k - lag >= 0, None)
                with eng.Fori(2, GPB // 2) as s:
                    for u in range(2):
                        body(2 * s + u, u, lambda lag: True, None)
                with eng.Fori(GPB // 2, GPB) as s:
                    for u in range(2):
                        body(2 * s + u, u, lambda lag: True, None)
                with eng.Fori(2, B) as b:
                    if at_graph is not None:
                        at_graph(b)
                    with eng.Fori(0, GPB // 2) as s:
                        for u in range(2):
                            body(b * GPB + 2 * s + u, u, lambda lag: True, b - 1)
                for k in range(K, K + lags):
                    body(k, k % 2, lambda lag: 0 <= k - lag < K, B - 2)

            @block.sync
            def _(sp):
                def body(b, u, live):
                    b = b if isinstance(b, int) else sp.snap(b)
                    if is_later(b, 2):
                        sp.wait_ge(e_mm, (b - 1) * GPB)
                    for part in range(3):
                        src = parts[part, b] if isinstance(b, int) else parts[part, bass.ds(b, 1)].rearrange("o i j -> (o i) j")
                        dst = e_ring[2 * part:2 * part + 2, u * GPB * 512:(u + 1) * GPB * 512]
                        sp.dma_start(dst.rearrange("h (s c) -> h s c", c=512),
                                     src.rearrange("(s h r) j -> h s (r j)", h=2, r=HALF)).then_inc(e_in[u], 16)
                run_steps(sp, B, 0, body)

            @block.tensor
            def _(pe):
                def spread(k):
                    if is_later(k, 1):
                        pe.wait_ge(sq_ok, k)
                    start = (k % (2 * GPB)) * 512 if isinstance(k, int) else (k & (2 * GPB - 1)) * 512
                    nc.tensor.matmul(ps_e[:, :], half[:, :], cols(e_ring, start, 512), start=True, stop=True).then_inc(e_mm, 1)

                def first(k, u):
                    pe.wait_ge(g_ok, k + 1)
                    if is_later(k, 2):
                        pe.wait_ge(h_ok, k - 1)
                    nc.tensor.matmul(ps_v[:, u, 0:512], w1[0:NG, :], gauss[0:NG, u, :], start=True, stop=True)
                    nc.tensor.matmul(ps_v[:, u, 512:1024], w1[NG:P, :], gauss[NG:P, u, :], start=True, stop=True).then_inc(v_mm, 1)

                def second(k, u):
                    pe.wait_ge(h_ok, k + 1)
                    for side in range(2):
                        if is_later(k, 1):
                            pe.wait_ge(z_ok, 2 * k - 1 + side)
                        for i in range(HALF):
                            c = (side * HALF + i) * P
                            last = nc.tensor.matmul(ps_w[:, side, i * P:(i + 1) * P], h[:, u, c:c + P], wt[:, W2T, :],
                                                    start=True, stop=True)
                        last.then_inc(w_mm, 1)

                def gather(k, u):
                    pe.wait_ge(z_ok, 2 * k + 2)
                    y0 = (k % (YRING * GPB)) * ROWS if isinstance(k, int) else (k & (YRING * GPB - 1)) * ROWS
                    for i in range(ROWS):
                        last = nc.tensor.matmul(cols(ps_y, y0 + i, 1), zt[:, u, i * P:(i + 1) * P], cols(adj_t, k * ROWS + i, 1),
                                                start=True, stop=True)
                    last.then_inc(y_mm, 1)

                def body(k, u, live, evacuated):
                    v = 1 - u
                    if live(1):
                        first(k - 1, v)
                    if live(0):
                        wait_e(k)
                        spread(k)
                    if live(3):
                        second(k - 3, v)
                    if live(4):
                        if evacuated is not None:
                            pe.wait_ge(y_ev, evacuated)
                        gather(k - 4, u)

                def wait_e(k):
                    if isinstance(k, int):
                        if k == 0:
                            pe.wait_ge(e_in[0], 48)
                        return
                    pe.wait_ge(e_in[0], ((k + 2 * GPB) >> 5) * 48)
                    pe.wait_ge(e_in[1], ((k + GPB) >> 5) * 48)

                all_groups(pe, 4, body)

            @block.scalar
            def _(act):
                def body(k, u, live, evacuated):
                    v = 1 - u
                    if live(0):
                        act.wait_ge(e_mm, k + 1)
                        nc.scalar.activation(dist2[:, :], ps_e[:, :], ACT.Square, bias=col[:, C_NOFF:C_NOFF + 1]).then_inc(sq_ok, 1)
                        act.wait_ge(sq_ok, k + 1)
                        if is_later(k, 2):
                            act.wait_ge(v_mm, k - 1)
                        nc.scalar.activation(gauss[:, u, :], dist2[:, :], ACT.Exp, scale=coeff).then_inc(g_ok, 1)
                    if live(1):
                        j = k - 1
                        act.wait_ge(v_mm, j + 1)
                        if is_later(j, 2):
                            act.wait_ge(h_ok, j - 1)
                        nc.scalar.activation(ex[:, v, :], ps_v[:, v, :], ACT.Exp, bias=col[:, C_B1:C_B1 + 1]).then_inc(ev_ok, 1)
                    if live(2):
                        act.wait_ge(cap_ok, k - 1)
                        nc.scalar.activation(ex[:, u, :], ex[:, u, :], ACT.Ln, scale=0.5, bias=0.5).then_inc(ln_ok, 1)
                nc.scalar.preload_act_table_set("natural_log_exp_and_others")
                all_groups(act, 2, body)

            @block.vector
            def _(dve):
                def evacuate(b, gathered):
                    dve.wait_ge(y_mm, gathered)
                    slot = (b % YRING) * P if isinstance(b, int) else (b & (YRING - 1)) * P
                    nc.vector.tensor_tensor(at(y_all, b), cols(ps_y, slot, P), at(y_all, b), ALU.add).then_inc(y_ev, 1)

                def body(k, u, live, evacuated):
                    v = 1 - u
                    if live(3):
                        j = k - 3
                        g = j // GPB if isinstance(j, int) else j // GPB
                        rf = at(rf_all, g).unsqueeze(1).to_broadcast([P, HALF, P])
                        for side in range(2):
                            dve.wait_ge(w_mm, 2 * j + 1 + side)
                            if side == 0 and is_later(j, 2):
                                dve.wait_ge(y_mm, j - 1)
                            nc.vector.tensor_tensor(zt[:, v, side * 512:(side + 1) * 512].rearrange("p (i f) -> p i f", f=P),
                                                    ps_w[:, side, :].rearrange("p (i f) -> p i f", f=P), rf, ALU.mult).then_inc(z_ok, 1)
                    if live(1):
                        j = k - 1
                        dve.wait_ge(ev_ok, j + 1)
                        nc.vector.tensor_scalar_min(ex[:, v, :], ex[:, v, :], EXP_CAP).then_inc(cap_ok, 1)
                    if live(2):
                        j = k - 2
                        dve.wait_ge(ln_ok, j + 1)
                        if is_later(j, 2):
                            dve.wait_ge(w_mm, 2 * (j - 1))
                        nc.vector.scalar_tensor_tensor(h[:, u, :], ps_v[:, u, :], b1_ln2[:, 0:1], ex[:, u, :],
                                                       ALU.add, ALU.max).then_inc(h_ok, 1)

                all_groups(dve, 4, body, lambda b: evacuate(b - 2, b * GPB - 4))
                for b in range(B - 2, B):
                    evacuate(b, K)

        Q = 4
        with ExitStack() as cx, nc.Block() as block:
            def tmp(name, shape, dt=F32):
                return cx.enter_context(nc.sbuf_tensor("l3e_" + name, shape, dt))

            def ps(name):
                return cx.enter_context(nc.psum_tensor("l3e_" + name, [P, 2, 512], F32))

            ex, s, t_o = (tmp(n, [P, 2, Q * P]) for n in ("ex", "s", "t"))
            ps_d, ps_o = ps("ps_d"), ps("ps_o")
            d_mm, ev_ok, cap_ok, ln_ok, s_ok, o_mm, t_ok, r_ok = (
                cx.enter_context(nc.semaphore("l3e_" + n))
                for n in ("d_mm", "ev_ok", "cap_ok", "ln_ok", "s_ok", "o_mm", "t_ok", "r_ok"))

            @block.tensor
            def _(pe):
                for c in range(B // Q):
                    u = c % 2
                    if c >= 2:
                        pe.wait_ge(s_ok, c - 1)
                    nc.tensor.matmul(ps_d[:, u, :], wt[:, WD1T, :], y_all[:, c * Q * P:(c + 1) * Q * P], start=True, stop=True).then_inc(d_mm, 1)
                    pe.wait_ge(s_ok, c + 1)
                    if c >= 2:
                        pe.wait_ge(t_ok, c - 1)
                    for q in range(Q):
                        last = nc.tensor.matmul(ps_o[:, u, q * P:(q + 1) * P], s[:, u, q * P:(q + 1) * P], wt[:, WD2T, :],
                                                start=True, stop=True)
                    last.then_inc(o_mm, 1)

            @block.scalar
            def _(act):
                for c in range(B // Q):
                    u = c % 2
                    act.wait_ge(d_mm, c + 1)
                    if c >= 2:
                        act.wait_ge(s_ok, c - 1)
                    nc.scalar.activation(ex[:, u, :], ps_d[:, u, :], ACT.Exp, bias=col[:, C_BD1:C_BD1 + 1]).then_inc(ev_ok, 1)
                    act.wait_ge(cap_ok, c + 1)
                    nc.scalar.activation(ex[:, u, :], ex[:, u, :], ACT.Ln, scale=0.5, bias=0.5).then_inc(ln_ok, 1)

            @block.vector
            def _(dve):
                for c in range(B // Q):
                    u = c % 2
                    dve.wait_ge(ev_ok, c + 1)
                    nc.vector.tensor_scalar_min(ex[:, u, :], ex[:, u, :], EXP_CAP).then_inc(cap_ok, 1)
                    dve.wait_ge(ln_ok, c + 1)
                    if c >= 2:
                        dve.wait_ge(o_mm, c - 1)
                    nc.vector.scalar_tensor_tensor(s[:, u, :], ps_d[:, u, :], bd1_ln2[:, 0:1], ex[:, u, :],
                                                   ALU.add, ALU.max).then_inc(s_ok, 1)
                    dve.wait_ge(o_mm, c + 1)
                    chunk = x_all[:, c * Q * P:(c + 1) * Q * P].rearrange("p (q e) -> p q e", e=P)
                    to3 = t_o[:, u, :].rearrange("p (q e) -> p q e", e=P)
                    nc.vector.tensor_tensor(to3, ps_o[:, u, :].rearrange("p (q e) -> p q e", e=P),
                                            row[:, R_BD2, :].unsqueeze(1).to_broadcast([P, Q, P]), ALU.add).then_inc(t_ok, 1)
                    dve.wait_ge(t_ok, c + 1)
                    nc.vector.tensor_tensor(chunk, to3, chunk, ALU.add).then_inc(r_ok, 1)
                    dve.wait_ge(r_ok, c + 1)
                    for q in range(Q):
                        row_stats(c * Q + q)

        rstd_phase("ln3")

        with ExitStack() as cx, nc.Block() as block:
            n_ok = cx.enter_context(nc.semaphore("out_n_ok"))
            stored = cx.enter_context(nc.semaphore("stored"))

            @block.vector
            def _(dve):
                with dve.Fori(0, B) as b:
                    normalise(at(x_all, b), at(x_all, b), b).then_inc(n_ok, 1)

            @block.sync
            def _(sp):
                for c in range(B // Q):
                    sp.wait_ge(n_ok, (c + 1) * Q)
                    sp.dma_start(out[c * Q:(c + 1) * Q].rearrange("b n d -> n b d"),
                                 x_all[:, c * Q * P:(c + 1) * Q * P].rearrange("p (b d) -> p b d", d=P)).then_inc(stored, 16)
                sp.wait_ge(stored, 16 * (B // Q))


def kernel(**inputs):
    import numpy as _np
    import concourse.bacc as _bacc
    from concourse import mybir as _mybir
    from concourse.bass_utils import run_bass_kernel_spmd as _run

    g = {n: _np.asarray(a) for n, a in inputs.items()}
    n_graphs = g["x"].shape[0]
    eye = _np.eye(P, dtype=_np.float32)
    off = _np.linspace(0.0, CUTOFF, NG, dtype=_np.float32)
    neg_offsets = _np.concatenate([-off, -off])
    side_of_row = _np.tile(_np.repeat(_np.eye(2, dtype=_np.float32), P // 2, axis=1), (3, 1))
    l1 = {n[len("L1_gnn_"):]: a for n, a in g.items() if n.startswith("L1_gnn_")}
    l3 = {n[len("L3_gnn_"):]: a for n, a in g.items() if n.startswith("L3_gnn_")}
    host = {
        "x": g["x"],
        "adj": g["adj"],
        "adjt": g["adj"].transpose(0, 2, 1),
        "weights": _np.stack([g["L0_gnn_W"].T, l1["W_ir"], l1["W_iz"], l1["W_im"], l1["W_xr"], l1["W_xz"], l1["W_xm"],
                              l1["W_hr"], l1["W_hz"], l1["W_hm"], g["L2_gnn_theta"], l3["Wa"].T, l3["W2"].T,
                              l3["Wd1"].T, l3["Wd2"].T, eye, 1 - eye], axis=1),
        "w1t": l3["W1"].T,
        "columns": _np.stack([l1["b_xr"], l1["b_hr"], l1["b_xz"], l1["b_hz"], l1["b_xm"], l1["b_hm"],
                              l3["b1"], l3["b2"], l3["bd1"], neg_offsets], axis=1),
        "rows": _np.stack([g["L0_gnn_b"], l1["b_ir"], l1["b_iz"], l1["b_im"], g["L2_gnn_bias"], l3["bd2"]], axis=0),
        "halves": side_of_row,
    }
    nc = _bacc.Bacc("TRN2", target_bir_lowering=False, num_devices=1)
    arrays, args = {}, []
    for name, a in host.items():
        a = _np.ascontiguousarray(a)
        arrays[f"in_{name}_dram"] = a
        args.append(nc.dram_tensor(f"in_{name}_dram", a.shape, _mybir.dt.from_np(a.dtype), kind="ExternalInput").ap())
    out = nc.dram_tensor("out_dram", g["x"].shape, _mybir.dt.float32, kind="ExternalOutput").ap()
    parts = nc.dram_tensor("adj_parts_dram", (3, n_graphs, P, P), _mybir.dt.bfloat16).ap()
    build(nc, n_graphs, *args, out, parts)
    r = _run(nc, [arrays], core_ids=[0])
    return r.results[0]["out_dram"]
```

```python
from contextlib import ExitStack

import numpy as np

import concourse.bass as bass
from concourse import mybir

ALU = mybir.AluOpType
ACT = mybir.ActivationFunctionType
AX_X = mybir.AxisListType.X
F32 = mybir.dt.float32
BF16 = mybir.dt.bfloat16

P = 128
NG = 64
CUTOFF = 5.0
LN2 = float(np.log(2.0))
LN_EPS = 1e-5
DEG_EPS = 1e-6
EXP_CAP = 2.0 ** 60

(W0T, WIR, WIZ, WIM, WXR, WXZ, WXM, WHR, WHZ, WHM, THETA, WAT, W2T, WD1T, WD2T, IDENT, OFFD) = range(17)
(C_XR, C_HR, C_XZ, C_HZ, C_XM, C_HM, C_B1, C_B2, C_BD1, C_NOFF) = range(10)
(R_B0, R_IR, R_IZ, R_IM, R_BIAS2, R_BD2) = range(6)

ROWS = 8
HALF = ROWS // 2
GPB = P // ROWS


def is_later(k, d):
    return k >= d if isinstance(k, int) else True


def run_steps(eng, total, lags, body):
    for k in range(min(4, total)):
        body(k, k % 2, lambda lag: k - lag >= 0)
    if total > 4:
        with eng.Fori(2, total // 2) as i:
            for u in range(2):
                body(2 * i + u, u, lambda lag: True)
    for k in range(total, total + lags):
        body(k, k % 2, lambda lag: 0 <= k - lag < total)


def build(nc, B, x, adj, adjt, weights, w1t, columns, rows, halves, out, parts):
    offsets = np.linspace(0.0, CUTOFF, NG, dtype=np.float32)
    width = offsets[1] - offsets[0]
    coeff = float(np.float32(-0.5) / (width * width))

    ctx = ExitStack()
    with ctx:
        def sb(name, shape, dt=F32):
            return ctx.enter_context(nc.sbuf_tensor(name, shape, dt))

        def sem(name):
            return ctx.enter_context(nc.semaphore(name))

        x_all = sb("x_all", [P, B * P])
        adj_t = sb("adj_t", [P, B * P])
        big = sb("big", [P, 3 * B * P])
        wt = sb("wt", [P, 17, P])
        w1 = sb("w1", [P, P])
        w1_hi = sb("w1_hi", [P, P], BF16)
        w1_lo = sb("w1_lo", [P, P], BF16)
        col = sb("col", [P, 10])
        row = sb("row", [P, 6, P])
        half_f = sb("half_f", [6, P])
        half = sb("half", [6, P], BF16)
        b_gate = sb("b_gate", [P, 2])
        b1_ln2 = sb("b1_ln2", [P, 1])
        bd1_ln2 = sb("bd1_ln2", [P, 1])
        deg = sb("deg", [P, 2, B])
        root = sb("root", [P, 2, B])
        dinv = sb("dinv", [P, 2, B])
        mean = sb("mean", [P, B])
        part_sq = sb("part_sq", [P, 2, B])
        var_eps = sb("var_eps", [P, B])
        std = sb("std", [P, B])
        rstd = sb("rstd", [P, B])
        six = sb("six", [P, B, 6])

        ident = wt[:, IDENT, :]

        def at(t, b):
            return t[:, b * P:(b + 1) * P] if isinstance(b, int) else t[:, bass.ds(b * P, P)]

        def column(t, b):
            return t[:, b:b + 1] if isinstance(b, int) else t[:, bass.ds(b, 1)]

        CH = min(8, B)
        with ExitStack() as cx, nc.Block() as block:
            s_w, s_x, s_at, s_an = (cx.enter_context(nc.semaphore(n)) for n in ("ld_w", "ld_x", "ld_adj_t", "ld_adj"))
            deg_sum = cx.enter_context(nc.semaphore("deg_sum"))
            deg_sh = cx.enter_context(nc.semaphore("deg_shifted"))
            root_ok = cx.enter_context(nc.semaphore("root_ok"))
            w1_hi_ok = cx.enter_context(nc.semaphore("w1_hi_ok"))
            adj_n = big[:, 0:B * P]

            @block.sync
            def _(sp):
                sp.dma_start(adj_n.rearrange("p (b j) -> p b j", j=P), adj.rearrange("b i j -> i b j")).then_inc(s_an, 16)
                sp.dma_start(x_all[:, :].rearrange("p (b j) -> p b j", j=P), x.rearrange("b i j -> i b j")).then_inc(s_x, 16)
                sp.dma_start(adj_t[:, :].rearrange("p (b j) -> p b j", j=P), adjt.rearrange("b i j -> i b j")).then_inc(s_at, 16)
                sp.wait_ge(s_an, 16)
                sp.wait_ge(s_x, 16)
                sp.wait_ge(s_at, 16)

            @block.scalar
            def _(act):
                act.dma_start(wt[:, :, :], weights).then_inc(s_w, 16)
                act.dma_start(w1[0:NG, :], w1t).then_inc(s_w, 16)
                act.dma_start(w1[NG:P, :], w1t).then_inc(s_w, 16)
                act.dma_start(col[:, :], columns).then_inc(s_w, 16)
                act.dma_start(row[:, :, :], rows.partition_broadcast(P)).then_inc(s_w, 16)
                act.dma_start(half_f[:, :], halves).then_inc(s_w, 16)
                act.wait_ge(deg_sh, 2)
                nc.scalar.activation(root[:, :, :], deg[:, :, :], ACT.Sqrt).then_inc(root_ok, 1)

            @block.vector
            def _(dve):
                dve.wait_ge(s_an, 16)
                nc.vector.tensor_reduce(deg[:, 0, :], adj_n.rearrange("p (b j) -> p b j", j=P), axis=AX_X, op=ALU.add).then_inc(deg_sum, 1)
                dve.wait_ge(deg_sum, 1)
                nc.vector.tensor_scalar_add(deg[:, 1, :], deg[:, 0, :], 1.0).then_inc(deg_sh, 1)
                dve.wait_ge(deg_sh, 1)
                nc.vector.tensor_scalar_add(deg[:, 0, :], deg[:, 1, :], DEG_EPS).then_inc(deg_sh, 1)
                dve.wait_ge(s_w, 96)
                nc.vector.tensor_copy(half[:, :], half_f[:, :])
                nc.vector.tensor_copy(w1_hi[:, :], w1[:, :]).then_inc(w1_hi_ok, 1)
                dve.wait_ge(w1_hi_ok, 1)
                nc.vector.tensor_tensor(w1_lo[:, :], w1[:, :], w1_hi[:, :], ALU.subtract)
                nc.vector.tensor_tensor(b_gate[:, 0:1], col[:, C_XR:C_XR + 1], col[:, C_HR:C_HR + 1], ALU.add)
                nc.vector.tensor_tensor(b_gate[:, 1:2], col[:, C_XZ:C_XZ + 1], col[:, C_HZ:C_HZ + 1], ALU.add)
                nc.vector.tensor_scalar_add(b1_ln2[:, :], col[:, C_B1:C_B1 + 1], -LN2)
                nc.vector.tensor_scalar_add(bd1_ln2[:, :], col[:, C_BD1:C_BD1 + 1], -LN2)
                dve.wait_ge(root_ok, 1)
                nc.vector.reciprocal(dinv[:, :, :], root[:, :, :])

        def rstd_phase(name):
            with ExitStack() as cx, nc.Block() as block:
                step = cx.enter_context(nc.semaphore(name + "_step"))
                ve_ok = cx.enter_context(nc.semaphore(name + "_var_eps"))
                std_ok = cx.enter_context(nc.semaphore(name + "_std"))

                @block.vector
                def _(dve):
                    nc.vector.tensor_tensor(mean[:, :], six[:, :, 1], six[:, :, 4], ALU.add).then_inc(step, 1)
                    nc.vector.tensor_tensor(part_sq[:, 0, :], six[:, :, 1], six[:, :, 4], ALU.subtract).then_inc(step, 1)
                    nc.vector.tensor_tensor(var_eps[:, :], six[:, :, 2], six[:, :, 5], ALU.add).then_inc(step, 1)
                    dve.wait_ge(step, 3)
                    nc.vector.tensor_scalar(mean[:, :], mean[:, :], 0.5, None, ALU.mult)
                    nc.vector.tensor_tensor(part_sq[:, 1, :], part_sq[:, 0, :], part_sq[:, 0, :], ALU.mult).then_inc(step, 1)
                    nc.vector.tensor_scalar(var_eps[:, :], var_eps[:, :], 1.0 / P, LN_EPS, ALU.mult, ALU.add).then_inc(step, 1)
                    dve.wait_ge(step, 5)
                    nc.vector.scalar_tensor_tensor(var_eps[:, :], part_sq[:, 1, :], 0.25, var_eps[:, :], ALU.mult, ALU.add).then_inc(ve_ok, 1)
                    dve.wait_ge(std_ok, 1)
                    nc.vector.reciprocal(rstd[:, :], std[:, :])

                @block.scalar
                def _(act):
                    act.wait_ge(ve_ok, 1)
                    nc.scalar.activation(std[:, :], var_eps[:, :], ACT.Sqrt).then_inc(std_ok, 1)

        def normalise(dst, src, b):
            return nc.vector.tensor_scalar(dst, src, column(mean, b),
                                           column(rstd, b), ALU.subtract, ALU.mult)

        def row_stats(b):
            dst = six[:, b, :] if isinstance(b, int) else six[:, bass.ds(b, 1), :].rearrange("p a c -> p (a c)")
            nc.vector.bn_stats(dst, at(x_all, b))

        with ExitStack() as cx, nc.Block() as block:
            def tmp(name, shape, dt=F32):
                return cx.enter_context(nc.sbuf_tensor("l0_" + name, shape, dt))

            def ps(name):
                return cx.enter_context(nc.psum_tensor("l0_" + name, [P, 2, 512], F32))

            ah, xs, st, t_o = (tmp(n, [P, 2, P]) for n in ("ah", "xs", "st", "t"))
            ps_s, ps_o = ps("ps_s"), ps("ps_o")
            ah_ok, xs_ok, s_ok, st_ok, o_ok, t_ok, r_ok = (
                cx.enter_context(nc.semaphore("l0_" + n))
                for n in ("ah_ok", "xs_ok", "s_ok", "st_ok", "o_ok", "t_ok", "r_ok"))

            @block.gpsimd
            def _(pool):
                def body(b, u, live):
                    if is_later(b, 2):
                        pool.wait_ge(s_ok, b - 1)
                    nc.gpsimd.tensor_tensor(ah[:, u, :], at(adj_t, b), ident, ALU.add).then_inc(ah_ok, 1)
                run_steps(pool, B, 0, body)

            @block.tensor
            def _(pe):
                def body(b, u, live):
                    if live(0):
                        pe.wait_ge(ah_ok, b + 1)
                        pe.wait_ge(xs_ok, b + 1)
                        if is_later(b, 2):
                            pe.wait_ge(st_ok, b - 1)
                        nc.tensor.matmul(ps_s[:, u, 0:P], xs[:, u, :], ah[:, u, :], start=True, stop=True).then_inc(s_ok, 1)
                    if live(1):
                        c, v = b - 1, 1 - u
                        pe.wait_ge(st_ok, c + 1)
                        if is_later(c, 2):
                            pe.wait_ge(t_ok, c - 1)
                        nc.tensor.matmul(ps_o[:, v, 0:P], st[:, v, :], wt[:, W0T, :], start=True, stop=True).then_inc(o_ok, 1)
                run_steps(pe, B, 1, body)

            @block.scalar
            def _(act):
                def body(b, u, live):
                    act.wait_ge(s_ok, b + 1)
                    if is_later(b, 2):
                        act.wait_ge(o_ok, b - 1)
                    nc.scalar.copy(st[:, u, :], ps_s[:, u, 0:P]).then_inc(st_ok, 1)
                run_steps(act, B, 0, body)

            @block.vector
            def _(dve):
                def body(b, u, live):
                    if live(0):
                        if is_later(b, 2):
                            dve.wait_ge(s_ok, b - 1)
                        nc.vector.tensor_scalar(xs[:, u, :], at(x_all, b), column(dinv[:, 0, :], b), None, ALU.mult).then_inc(xs_ok, 1)
                    if live(2):
                        dve.wait_ge(r_ok, b - 1)
                    if live(1):
                        c, v = b - 1, 1 - u
                        dve.wait_ge(o_ok, c + 1)
                        nc.vector.scalar_tensor_tensor(t_o[:, v, :], ps_o[:, v, 0:P], column(dinv[:, 0, :], c), row[:, R_B0, :],
                                                       ALU.mult, ALU.add).then_inc(t_ok, 1)
                    if live(2):
                        row_stats(b - 2)
                    if live(1):
                        dve.wait_ge(t_ok, c + 1)
                        nc.vector.scalar_tensor_tensor(at(x_all, c), t_o[:, v, :], 0.0, at(x_all, c), ALU.max, ALU.add).then_inc(r_ok, 1)
                run_steps(dve, B, 2, body)

        rstd_phase("ln0")

        gates = big[:, :].rearrange("p (t c b) -> p t c b", c=3, b=B)
        with ExitStack() as cx, nc.Block() as block:
            def tmp(name, shape, dt=F32):
                return cx.enter_context(nc.sbuf_tensor("l1_" + name, shape, dt))

            def ps(name):
                return cx.enter_context(nc.psum_tensor("l1_" + name, [P, 2, 512], F32))

            x1, x1t, gt = (tmp(n, [P, 2, P]) for n in ("x1", "x1t", "gt"))
            proj = tmp("proj", [P, 2, 3 * P])
            ps_t, ps_p, ps_a = ps("ps_t"), ps("ps_p"), ps("ps_a")
            n_ok, cp_ok, g_ok, t_ok, xt_ok, p_ok, pj_ok, a_ok, ev_ok = (
                cx.enter_context(nc.semaphore("l1_" + n))
                for n in ("n_ok", "cp_ok", "g_ok", "t_ok", "xt_ok", "p_ok", "pj_ok", "a_ok", "ev_ok"))

            @block.gpsimd
            def _(pool):
                def body(b, u, live):
                    if is_later(b, 2):
                        pool.wait_ge(a_ok, b - 1)
                    pool.wait_ge(n_ok, b + 1)
                    nc.gpsimd.tensor_tensor(gt[:, u, :], at(adj_t, b), wt[:, OFFD, :], ALU.mult).then_inc(g_ok, 1)
                    nc.gpsimd.tensor_copy(at(x_all, b), x1[:, u, :]).then_inc(cp_ok, 1)
                run_steps(pool, B, 0, body)

            @block.vector
            def _(dve):
                def body(b, u, live):
                    if live(0):
                        if is_later(b, 2):
                            dve.wait_ge(t_ok, b - 1)
                            dve.wait_ge(cp_ok, b - 1)
                        normalise(x1[:, u, :], at(x_all, b), b).then_inc(n_ok, 1)
                    if live(1):
                        c, v = b - 1, 1 - u
                        dve.wait_ge(p_ok, c + 1)
                        if is_later(c, 2):
                            dve.wait_ge(a_ok, c - 1)
                        nc.vector.tensor_tensor(proj[:, v, :], ps_p[:, v, 0:3 * P],
                                                row[:, R_IR:R_IM + 1, :].rearrange("p a b -> p (a b)"), ALU.add).then_inc(pj_ok, 1)
                run_steps(dve, B, 1, body)

            @block.tensor
            def _(pe):
                def body(b, u, live):
                    if live(0):
                        pe.wait_ge(n_ok, b + 1)
                        if is_later(b, 2):
                            pe.wait_ge(xt_ok, b - 1)
                        nc.tensor.transpose(ps_t[:, u, 0:P], x1[:, u, :], ident).then_inc(t_ok, 1)
                    if live(2):
                        c = b - 2
                        pe.wait_ge(pj_ok, c + 1)
                        pe.wait_ge(g_ok, c + 1)
                        if is_later(c, 2):
                            pe.wait_ge(ev_ok, 3 * (c - 1))
                        for a in range(3):
                            nc.tensor.matmul(ps_a[:, u, a * P:(a + 1) * P], wt[:, WXR + a, :], x1t[:, u, :], start=True, stop=False)
                            last = nc.tensor.matmul(ps_a[:, u, a * P:(a + 1) * P], proj[:, u, a * P:(a + 1) * P], gt[:, u, :],
                                                    start=False, stop=True)
                        last.then_inc(a_ok, 1)
                    if live(1):
                        c, v = b - 1, 1 - u
                        pe.wait_ge(xt_ok, c + 1)
                        if is_later(c, 2):
                            pe.wait_ge(pj_ok, c - 1)
                        nc.tensor.matmul(ps_p[:, v, 0:3 * P], x1t[:, v, :], wt[:, WIR:WIM + 1, :].rearrange("p a b -> p (a b)"),
                                         start=True, stop=True).then_inc(p_ok, 1)
                run_steps(pe, B, 2, body)

            @block.scalar
            def _(act):
                def body(b, u, live):
                    if live(2):
                        c = b - 2
                        act.wait_ge(a_ok, c + 1)
                        for a, bias in enumerate((b_gate[:, 0:1], b_gate[:, 1:2], col[:, C_XM:C_XM + 1])):
                            dst = gates[:, :, a, c] if isinstance(c, int) else gates[:, :, a, bass.ds(c, 1)].rearrange("p t o -> p (t o)")
                            nc.scalar.activation(dst, ps_a[:, u, a * P:(a + 1) * P], ACT.Identity, bias=bias).then_inc(ev_ok, 1)
                    if live(0):
                        act.wait_ge(t_ok, b + 1)
                        if is_later(b, 2):
                            act.wait_ge(a_ok, b - 1)
                        nc.scalar.copy(x1t[:, u, :], ps_t[:, u, 0:P]).then_inc(xt_ok, 1)
                run_steps(act, B, 2, body)

        with ExitStack() as cx, nc.Block() as block:
            def tmp(name, shape, dt=F32):
                return cx.enter_context(nc.sbuf_tensor("gru_" + name, shape, dt))

            def ps(name):
                return cx.enter_context(nc.psum_tensor("gru_" + name, [P, 2, 512], F32))

            r, z, m, t1, t2, omz, zh, om = (tmp(n, [P, 2, B]) for n in ("r", "z", "m", "t1", "t2", "omz", "zh", "om"))
            zero = tmp("zero", [P, B])
            CUT = 2
            an = tmp("an", [P, 2, CUT * P])
            rest = tmp("rest", [P, 2, CUT * P])
            cut = tmp("cut", [P, 2, 3, CUT * P], BF16)
            ps_r, ps_z, ps_m = ps("ps_r"), ps("ps_z"), ps("ps_m")
            (init_ok, r_mm, m_mm, z_mm, r_s, z_s, m_s, t1_ok, t2_ok, zh_ok, omz_ok, om_ok, h_ok) = (
                cx.enter_context(nc.semaphore("gru_" + n))
                for n in ("init", "r_mm", "m_mm", "z_mm", "r_s", "z_s", "m_s", "t1_ok", "t2_ok", "zh_ok", "omz_ok", "om_ok", "h_ok"))
            an_in = [cx.enter_context(nc.semaphore(f"cut_in{u}")) for u in range(2)]
            cut_out = [cx.enter_context(nc.semaphore(f"cut_out{u}")) for u in range(2)]
            cut_step = cx.enter_context(nc.semaphore("cut_step"))

            @block.vector
            def _(dve):
                nc.vector.memset(zero[:, :], 0.0).then_inc(init_ok, 1)
                nc.vector.memset(zh[:, 1, :], 0.0).then_inc(init_ok, 1)
                nc.vector.memset(om[:, 1, :], 0.0).then_inc(init_ok, 1)
                dve.wait_ge(init_ok, 3)

                def body(t, u, live):
                    g = gates[:, t, :, :] if isinstance(t, int) else gates[:, bass.ds(t, 1), :, :].rearrange("p o c b -> p (o c) b")
                    if isinstance(t, int):
                        before = zero[:, :] if t == 0 else gates[:, t - 1, 0, :]
                    else:
                        before = gates[:, bass.ds(t - 1, 1), 0, :].rearrange("p o b -> p (o b)")
                    dve.wait_ge(m_mm, t + 1)
                    dve.wait_ge(r_s, t + 1)
                    nc.vector.scalar_tensor_tensor(t1[:, u, :], ps_m[:, u, 0:B], col[:, C_HM:C_HM + 1], r[:, u, :],
                                                   ALU.add, ALU.mult).then_inc(t1_ok, 1)
                    dve.wait_ge(t1_ok, t + 1)
                    nc.vector.tensor_tensor(t2[:, u, :], t1[:, u, :], g[:, 2, :], ALU.add).then_inc(t2_ok, 1)
                    dve.wait_ge(z_s, t + 1)
                    if is_later(t, 1):
                        dve.wait_ge(h_ok, t)
                    nc.vector.tensor_tensor(zh[:, u, :], z[:, u, :], before, ALU.mult).then_inc(zh_ok, 1)
                    nc.vector.tensor_scalar(omz[:, u, :], z[:, u, :], -1.0, 1.0, ALU.mult, ALU.add).then_inc(omz_ok, 1)
                    dve.wait_ge(omz_ok, t + 1)
                    dve.wait_ge(m_s, t + 1)
                    nc.vector.tensor_tensor(om[:, u, :], omz[:, u, :], m[:, u, :], ALU.mult).then_inc(om_ok, 1)
                    dve.wait_ge(zh_ok, t + 1)
                    dve.wait_ge(om_ok, t + 1)
                    nc.vector.tensor_tensor(g[:, 0, :], om[:, u, :], zh[:, u, :], ALU.add).then_inc(h_ok, 1)
                run_steps(dve, P, 0, body)

            @block.scalar
            def _(act):
                def body(t, u, live):
                    act.wait_ge(r_mm, t + 1)
                    nc.scalar.activation(r[:, u, :], ps_r[:, u, 0:B], ACT.Sigmoid).then_inc(r_s, 1)
                    act.wait_ge(z_mm, t + 1)
                    nc.scalar.activation(z[:, u, :], ps_z[:, u, 0:B], ACT.Sigmoid).then_inc(z_s, 1)
                    act.wait_ge(t2_ok, t + 1)
                    nc.scalar.activation(m[:, u, :], t2[:, u, :], ACT.Tanh).then_inc(m_s, 1)
                nc.scalar.preload_act_table_set("sigmoid_and_others")
                run_steps(act, P, 0, body)

            @block.tensor
            def _(pe):
                def seed(t, u):
                    for c, dst in enumerate((ps_r, ps_z)):
                        src = gates[:, t, c, :] if isinstance(t, int) else gates[:, bass.ds(t, 1), c, :].rearrange("p o b -> p (o b)")
                        nc.tensor.matmul(dst[:, u, 0:B], ident, src, start=True, stop=False)

                seed(0, 0)
                pe.wait_ge(init_ok, 3)

                def body(t, u, live):
                    v = 1 - u
                    if is_later(t, 1):
                        pe.wait_ge(zh_ok, t)
                    nc.tensor.matmul(ps_r[:, u, 0:B], wt[:, WHR, :], zh[:, v, :], start=False, stop=False)
                    nc.tensor.matmul(ps_m[:, u, 0:B], wt[:, WHM, :], zh[:, v, :], start=True, stop=False)
                    nc.tensor.matmul(ps_z[:, u, 0:B], wt[:, WHZ, :], zh[:, v, :], start=False, stop=False)
                    if is_later(t, 1):
                        pe.wait_ge(om_ok, t)
                    nc.tensor.matmul(ps_r[:, u, 0:B], wt[:, WHR, :], om[:, v, :], start=False, stop=True).then_inc(r_mm, 1)
                    nc.tensor.matmul(ps_m[:, u, 0:B], wt[:, WHM, :], om[:, v, :], start=False, stop=True).then_inc(m_mm, 1)
                    nc.tensor.matmul(ps_z[:, u, 0:B], wt[:, WHZ, :], om[:, v, :], start=False, stop=True).then_inc(z_mm, 1)
                    if not (isinstance(t, int) and t == P - 1):
                        seed(t + 1, v)
                for t in range(4):
                    body(t, t % 2, None)
                with pe.Fori(2, P // 2 - 1) as i:
                    for u in range(2):
                        body(2 * i + u, u, None)
                for t in range(P - 2, P):
                    body(t, t % 2, None)

            @block.sync
            def _(sp):
                for c in range(B // CUT + 1):
                    if c < B // CUT:
                        if c >= 2:
                            sp.wait_ge(cut_step, 5 * (c - 1))
                        sp.dma_start(an[:, c % 2, :].rearrange("i (b j) -> i b j", j=P),
                                     adj[c * CUT:(c + 1) * CUT].rearrange("b i j -> i b j")).then_inc(an_in[c % 2], 16)
                    if c >= 1:
                        sp.wait_ge(cut_step, 5 * c)
                        for part in range(3):
                            sp.dma_start(parts[part, (c - 1) * CUT:c * CUT].rearrange("b i j -> i b j"),
                                         cut[:, (c - 1) % 2, part, :].rearrange("i (b j) -> i b j", j=P)).then_inc(cut_out[(c - 1) % 2], 16)
                for u in range(2):
                    sp.wait_ge(cut_out[u], 48 * ((B // CUT + 1 - u) // 2))

            @block.gpsimd
            def _(pool):
                for c in range(B // CUT):
                    u = c % 2
                    pool.wait_ge(an_in[u], 16 * (c // 2 + 1))
                    if c >= 2:
                        pool.wait_ge(cut_out[u], 48 * (c // 2))
                    nc.gpsimd.tensor_copy(cut[:, u, 0, :], an[:, u, :]).then_inc(cut_step, 1)
                    pool.wait_ge(cut_step, 5 * c + 1)
                    nc.gpsimd.tensor_tensor(rest[:, u, :], an[:, u, :], cut[:, u, 0, :], ALU.subtract).then_inc(cut_step, 1)
                    pool.wait_ge(cut_step, 5 * c + 2)
                    nc.gpsimd.tensor_copy(cut[:, u, 1, :], rest[:, u, :]).then_inc(cut_step, 1)
                    pool.wait_ge(cut_step, 5 * c + 3)
                    nc.gpsimd.tensor_tensor(an[:, u, :], rest[:, u, :], cut[:, u, 1, :], ALU.subtract).then_inc(cut_step, 1)
                    pool.wait_ge(cut_step, 5 * c + 4)
                    nc.gpsimd.tensor_copy(cut[:, u, 2, :], an[:, u, :]).then_inc(cut_step, 1)

        with ExitStack() as cx, nc.Block() as block:
            hs = cx.enter_context(nc.sbuf_tensor("l1_hs", [P, 2, P], F32))
            ps_t = cx.enter_context(nc.psum_tensor("l1_ps_h", [P, 2, 512], F32))
            h_ok, t_ok, r_ok = (cx.enter_context(nc.semaphore("l1s_" + n)) for n in ("h_ok", "t_ok", "r_ok"))

            @block.scalar
            def _(act):
                def body(b, u, live):
                    if is_later(b, 2):
                        act.wait_ge(t_ok, b - 1)
                    src = gates[:, :, 0, b] if isinstance(b, int) else gates[:, :, 0, bass.ds(b, 1)].rearrange("p t o -> p (t o)")
                    nc.scalar.activation(hs[:, u, :], src, ACT.Relu).then_inc(h_ok, 1)
                run_steps(act, B, 0, body)

            @block.tensor
            def _(pe):
                def body(b, u, live):
                    pe.wait_ge(h_ok, b + 1)
                    if is_later(b, 2):
                        pe.wait_ge(r_ok, b - 1)
                    nc.tensor.transpose(ps_t[:, u, 0:P], hs[:, u, :], ident).then_inc(t_ok, 1)
                run_steps(pe, B, 0, body)

            @block.vector
            def _(dve):
                def body(b, u, live):
                    if live(1):
                        dve.wait_ge(r_ok, b)
                    if live(0):
                        dve.wait_ge(t_ok, b + 1)
                        nc.vector.tensor_tensor(at(x_all, b), ps_t[:, u, 0:P], at(x_all, b), ALU.add).then_inc(r_ok, 1)
                    if live(1):
                        row_stats(b - 1)
                run_steps(dve, B, 1, body)

        rstd_phase("ln1")

        with ExitStack() as cx, nc.Block() as block:
            def tmp(name, shape, dt=F32):
                return cx.enter_context(nc.sbuf_tensor("l2_" + name, shape, dt))

            def ps(name):
                return cx.enter_context(nc.psum_tensor("l2_" + name, [P, 2, 512], F32))

            x2, x2t, ah, sup, t_o = (tmp(n, [P, 2, P]) for n in ("x2", "x2t", "ah", "sup", "t"))
            ps_t, ps_u, ps_o = ps("ps_t"), ps("ps_u"), ps("ps_o")
            n_ok, cp_ok, ah_ok, t_ok, xt_ok, u_ok, sup_ok, o_ok, to_ok, r_ok = (
                cx.enter_context(nc.semaphore("l2_" + n))
                for n in ("n_ok", "cp_ok", "ah_ok", "t_ok", "xt_ok", "u_ok", "sup_ok", "o_ok", "to_ok", "r_ok"))

            @block.gpsimd
            def _(pool):
                def body(b, u, live):
                    if is_later(b, 2):
                        pool.wait_ge(o_ok, b - 1)
                    pool.wait_ge(n_ok, b + 1)
                    nc.gpsimd.tensor_tensor(ah[:, u, :], at(adj_t, b), ident, ALU.add).then_inc(ah_ok, 1)
                    nc.gpsimd.tensor_copy(at(x_all, b), x2[:, u, :]).then_inc(cp_ok, 1)
                run_steps(pool, B, 0, body)

            @block.tensor
            def _(pe):
                def body(b, u, live):
                    if live(0):
                        pe.wait_ge(n_ok, b + 1)
                        if is_later(b, 2):
                            pe.wait_ge(xt_ok, b - 1)
                        nc.tensor.transpose(ps_t[:, u, 0:P], x2[:, u, :], ident).then_inc(t_ok, 1)
                    if live(2):
                        c = b - 2
                        pe.wait_ge(sup_ok, c + 1)
                        pe.wait_ge(ah_ok, c + 1)
                        if is_later(c, 2):
                            pe.wait_ge(to_ok, c - 1)
                        nc.tensor.matmul(ps_o[:, u, 0:P], ah[:, u, :], sup[:, u, :], start=True, stop=True).then_inc(o_ok, 1)
                    if live(1):
                        c, v = b - 1, 1 - u
                        pe.wait_ge(xt_ok, c + 1)
                        if is_later(c, 2):
                            pe.wait_ge(sup_ok, c - 1)
                        nc.tensor.matmul(ps_u[:, v, 0:P], x2t[:, v, :], wt[:, THETA, :], start=True, stop=True).then_inc(u_ok, 1)
                run_steps(pe, B, 2, body)

            @block.scalar
            def _(act):
                def body(b, u, live):
                    if live(0):
                        act.wait_ge(t_ok, b + 1)
                        if is_later(b, 2):
                            act.wait_ge(u_ok, b - 1)
                        nc.scalar.copy(x2t[:, u, :], ps_t[:, u, 0:P]).then_inc(xt_ok, 1)
                    if live(1):
                        c, v = b - 1, 1 - u
                        act.wait_ge(u_ok, c + 1)
                        if is_later(c, 2):
                            act.wait_ge(o_ok, c - 1)
                        nc.scalar.activation(sup[:, v, :], ps_u[:, v, 0:P], ACT.Copy, scale=column(dinv[:, 1, :], c)).then_inc(sup_ok, 1)
                run_steps(act, B, 1, body)

            @block.vector
            def _(dve):
                def body(b, u, live):
                    if live(0):
                        if is_later(b, 2):
                            dve.wait_ge(t_ok, b - 1)
                            dve.wait_ge(cp_ok, b - 1)
                        normalise(x2[:, u, :], at(x_all, b), b).then_inc(n_ok, 1)
                    if live(3):
                        dve.wait_ge(r_ok, b - 2)
                    if live(2):
                        c = b - 2
                        dve.wait_ge(o_ok, c + 1)
                        nc.vector.scalar_tensor_tensor(t_o[:, u, :], ps_o[:, u, 0:P], column(dinv[:, 1, :], c), row[:, R_BIAS2, :],
                                                       ALU.mult, ALU.add).then_inc(to_ok, 1)
                    if live(3):
                        row_stats(b - 3)
                    if live(2):
                        dve.wait_ge(to_ok, c + 1)
                        dve.wait_ge(cp_ok, c + 1)
                        nc.vector.tensor_tensor(at(x_all, c), t_o[:, u, :], at(x_all, c), ALU.add).then_inc(r_ok, 1)
                run_steps(dve, B, 3, body)

        rstd_phase("ln2")

        rf_all = big[:, 0:B * P]
        y_all = big[:, B * P:2 * B * P]
        a2_parts = adj_t[:, :].bitcast(BF16)

        def a2_part(b, part):
            t = a2_parts.rearrange("p (c t) -> p t c", t=2)[:, part, :]
            return at(t, b)

        with ExitStack() as cx, nc.Block() as block:
            def tmp(name, shape, dt=F32):
                return cx.enter_context(nc.sbuf_tensor("l3p_" + name, shape, dt))

            def ps(name):
                return cx.enter_context(nc.psum_tensor("l3p_" + name, [P, 2, 512], F32))

            x3, x3t, rfs, a2 = (tmp(n, [P, 2, P]) for n in ("x3", "x3t", "rfs", "a2"))
            ps_t, ps_f, ps_q = ps("ps_t"), ps("ps_f"), ps("ps_q")
            n_ok, cp_ok, sq_ok, hi_ok, lo_ok, t_ok, xt_ok, f_ok, rfs_ok, rf_ok, q_ok, y_ok = (
                cx.enter_context(nc.semaphore("l3p_" + n))
                for n in ("n_ok", "cp_ok", "sq_ok", "hi_ok", "lo_ok", "t_ok", "xt_ok", "f_ok", "rfs_ok", "rf_ok", "q_ok", "y_ok"))

            @block.gpsimd
            def _(pool):
                def body(b, u, live):
                    pool.wait_ge(n_ok, b + 1)
                    if is_later(b, 2):
                        pool.wait_ge(q_ok, b - 1)
                        pool.wait_ge(lo_ok, b - 1)
                    nc.gpsimd.tensor_tensor(a2[:, u, :], at(adj_t, b), at(adj_t, b), ALU.mult).then_inc(sq_ok, 1)
                    nc.gpsimd.tensor_copy(at(x_all, b), x3[:, u, :]).then_inc(cp_ok, 1)
                run_steps(pool, B, 0, body)

            @block.tensor
            def _(pe):
                def body(b, u, live):
                    if live(0):
                        pe.wait_ge(n_ok, b + 1)
                        if is_later(b, 2):
                            pe.wait_ge(xt_ok, b - 1)
                        nc.tensor.transpose(ps_t[:, u, 0:P], x3[:, u, :], ident).then_inc(t_ok, 1)
                    if live(2):
                        c = b - 2
                        pe.wait_ge(rfs_ok, c + 1)
                        pe.wait_ge(sq_ok, c + 1)
                        if is_later(c, 2):
                            pe.wait_ge(y_ok, c - 1)
                        nc.tensor.matmul(ps_q[:, u, 0:P], rfs[:, u, :], a2[:, u, :], start=True, stop=True).then_inc(q_ok, 1)
                    if live(1):
                        c, v = b - 1, 1 - u
                        pe.wait_ge(xt_ok, c + 1)
                        if is_later(c, 2):
                            pe.wait_ge(rfs_ok, c - 1)
                        nc.tensor.matmul(ps_f[:, v, 0:P], x3t[:, v, :], wt[:, WAT, :], start=True, stop=True).then_inc(f_ok, 1)
                run_steps(pe, B, 2, body)

            @block.scalar
            def _(act):
                def body(b, u, live):
                    if live(0):
                        act.wait_ge(t_ok, b + 1)
                        if is_later(b, 2):
                            act.wait_ge(f_ok, b - 1)
                        nc.scalar.copy(x3t[:, u, :], ps_t[:, u, 0:P]).then_inc(xt_ok, 1)
                    if live(1):
                        c, v = b - 1, 1 - u
                        act.wait_ge(f_ok, c + 1)
                        if is_later(c, 2):
                            act.wait_ge(q_ok, c - 1)
                            act.wait_ge(rf_ok, c - 1)
                        nc.scalar.copy(rfs[:, v, :], ps_f[:, v, 0:P]).then_inc(rfs_ok, 1)
                run_steps(act, B, 1, body)

            @block.vector
            def _(dve):
                def body(b, u, live):
                    if live(0):
                        if is_later(b, 2):
                            dve.wait_ge(t_ok, b - 1)
                            dve.wait_ge(cp_ok, b - 1)
                        normalise(x3[:, u, :], at(x_all, b), b).then_inc(n_ok, 1)
                    if live(1):
                        c, v = b - 1, 1 - u
                        dve.wait_ge(rfs_ok, c + 1)
                        nc.vector.tensor_copy(at(rf_all, c), rfs[:, v, :]).then_inc(rf_ok, 1)
                        dve.wait_ge(sq_ok, c + 1)
                        nc.vector.tensor_tensor(a2_part(c, 0), a2[:, v, :], a2[:, v, :], ALU.max).then_inc(hi_ok, 1)
                        dve.wait_ge(hi_ok, c + 1)
                        nc.vector.tensor_tensor(a2_part(c, 1), a2[:, v, :], a2_part(c, 0), ALU.subtract).then_inc(lo_ok, 1)
                    if live(2):
                        c = b - 2
                        dve.wait_ge(q_ok, c + 1)
                        nc.vector.tensor_scalar(at(y_all, c), ps_q[:, u, 0:P], col[:, C_B2:C_B2 + 1], None, ALU.mult).then_inc(y_ok, 1)
                run_steps(dve, B, 2, body)

        GAUSS, FIRST, LN, SECOND, GATHER = 1, 3, 4, 5, 6
        HG = GPB // 2
        with ExitStack() as cx, nc.Block() as block:
            def tmp(name, shape, dt=F32):
                return cx.enter_context(nc.sbuf_tensor("l3_" + name, shape, dt))

            e_ring = tmp("e_ring", [6, 2, HG * 512], BF16)
            dist2 = tmp("dist2", [P, 2, 512])
            WORK = 8192
            work = big[:, 2 * B * P:2 * B * P + WORK] if B * P >= WORK else tmp("work", [P, WORK])[:, :]
            ex, h, zt = (work[:, n * 2048:(n + 1) * 2048].rearrange("p (u c) -> p u c", u=2) for n in range(3))
            gauss = work[:, 6144:7168].rearrange("p (u c) -> p u c", u=2)
            zl = work[:, 7168:8192].bitcast(BF16).rearrange("p (u c) -> p u c", u=2)
            z_upper = work[:, 4096:6144].bitcast(BF16).rearrange("p (u c t) -> p u c t", u=2, t=2)[:, :, :, 1]
            g_upper = work[:, 6144:7168].bitcast(BF16).rearrange("p (u c t) -> p u c t", u=2, t=2)[:, :, :, 1]
            gl = tmp("gl", [P, 2, 512], BF16)
            a2_half = tmp("a2_half", [P, HG * ROWS])
            a2_now = a2_half[:, :].bitcast(BF16)
            ps_e = cx.enter_context(nc.psum_tensor("l3_ps_e", [P, 512], F32))
            ps_v = cx.enter_context(nc.psum_tensor("l3_ps_v", [P, 2, 1024], F32))
            ps_w = cx.enter_context(nc.psum_tensor("l3_ps_w", [P, 2, 512], F32))
            ps_y = cx.enter_context(nc.psum_tensor("l3_ps_y", [P, 512], F32))
            (e_mm, sq_ok, g_ok, gl_ok, v_mm, ev_ok, cap_ok, ln_ok, h_ok, w_mm, z_ok, zl_ok, y_mm, y_half, y_ev, a2_in) = (
                cx.enter_context(nc.semaphore("l3_" + n))
                for n in ("e_mm", "sq_ok", "g_ok", "gl_ok", "v_mm", "ev_ok", "cap_ok", "ln_ok", "h_ok", "w_mm", "z_ok", "zl_ok", "y_mm",
                          "y_half", "y_ev", "a2_in"))
            e_in = [cx.enter_context(nc.semaphore(f"l3_e_in{u}")) for u in range(2)]

            def back(b, s, lag):
                c, r = (b, s - lag) if s >= lag else (b - 1, s - lag + GPB)
                return c, r, c * GPB + r

            def all_groups(eng, step):
                for s in range(GPB):
                    step(0, s, lambda lag: s - lag >= 0)
                with eng.Fori(1, B) as b:
                    for s in range(GPB):
                        step(b, s, lambda lag: True)
                for s in range(GATHER):
                    step(B, s, lambda lag: s < lag)

            @block.sync
            def _(sp):
                def load(b):
                    for side in range(2):
                        if is_later(b, 1):
                            sp.wait_ge(e_mm, (b - 1) * GPB + (side + 1) * HG)
                        for part in range(3):
                            src = parts[part, b] if isinstance(b, int) else parts[part, bass.ds(b, 1)].rearrange("o i j -> (o i) j")
                            src = src[side * HG * ROWS:(side + 1) * HG * ROWS]
                            sp.dma_start(e_ring[2 * part:2 * part + 2, side, :].rearrange("h (s c) -> h s c", c=512),
                                         src.rearrange("(s h r) j -> h s (r j)", h=2, r=HALF)).then_inc(e_in[side], 16)
                load(0)
                with sp.Fori(1, B) as b:
                    load(sp.snap(b))

            @block.tensor
            def _(pe):
                def spread(b, s, k):
                    if s % HG == 0:
                        pe.wait_ge(e_in[s // HG], 48 * (b + 1))
                    if is_later(k, 1):
                        pe.wait_ge(sq_ok, k)
                    nc.tensor.matmul(ps_e[:, :], half[:, :], e_ring[:, s // HG, s % HG * 512:(s % HG + 1) * 512],
                                     start=True, stop=True).then_inc(e_mm, 1)

                def first(k, u):
                    pe.wait_ge(gl_ok, k + 1)
                    if is_later(k, 2):
                        pe.wait_ge(h_ok, k - 1)
                    for side in range(2):
                        half_p = slice(side * NG, (side + 1) * NG)
                        v = ps_v[:, u, side * 512:(side + 1) * 512]
                        nc.tensor.matmul(v, w1_hi[half_p, :], g_upper[half_p, u, :], start=True, stop=False)
                        nc.tensor.matmul(v, w1_hi[half_p, :], gl[half_p, u, :], start=False, stop=False)
                        last = nc.tensor.matmul(v, w1_lo[half_p, :], g_upper[half_p, u, :], start=False, stop=True)
                    last.then_inc(v_mm, 1)

                def second(k, u):
                    pe.wait_ge(h_ok, k + 1)
                    for side in range(2):
                        if is_later(k, 1):
                            pe.wait_ge(z_ok, 2 * k - 1 + side)
                        for i in range(HALF):
                            c = (side * HALF + i) * P
                            last = nc.tensor.matmul(ps_w[:, side, i * P:(i + 1) * P], h[:, u, c:c + P], wt[:, W2T, :],
                                                    start=True, stop=True)
                        last.then_inc(w_mm, 1)

                def gather(b, s, k, u):
                    if s % HG == 0:
                        pe.wait_ge(a2_in, 2 * b + s // HG + 1)
                        if is_later(k, 1):
                            pe.wait_ge(y_ev, 2 * b + s // HG)
                    pe.wait_ge(zl_ok, k + 1)
                    for i in range(ROWS):
                        at_y = (s % HG * ROWS + i) * 2
                        nc.tensor.matmul(ps_y[:, at_y:at_y + 2], z_upper[:, u, i * P:(i + 1) * P], a2_now[:, at_y:at_y + 2],
                                         start=True, stop=False)
                        last = nc.tensor.matmul(ps_y[:, at_y:at_y + 2], zl[:, u, i * P:(i + 1) * P], a2_now[:, at_y:at_y + 2],
                                                start=False, stop=True)
                    last.then_inc(y_mm, 1)

                def step(b, s, live):
                    if live(FIRST):
                        first(back(b, s, FIRST)[2], (s - FIRST) % 2)
                    if live(SECOND):
                        second(back(b, s, SECOND)[2], (s - SECOND) % 2)
                    if live(GATHER):
                        gather(*back(b, s, GATHER), (s - GATHER) % 2)
                    if live(0):
                        spread(*back(b, s, 0))
                all_groups(pe, step)

            @block.gpsimd
            def _(pool):
                def step(b, s, live):
                    if live(GATHER):
                        j, u = back(b, s, GATHER)[2], (s - GATHER) % 2
                        pool.wait_ge(z_ok, 2 * j + 2)
                        if is_later(j, 2):
                            pool.wait_ge(y_mm, j - 1)
                        nc.gpsimd.tensor_tensor(zl[:, u, :], zt[:, u, :], z_upper[:, u, :], ALU.subtract).then_inc(zl_ok, 1)
                    if live(GAUSS):
                        k, u = back(b, s, GAUSS)[2], (s - GAUSS) % 2
                        pool.wait_ge(g_ok, k + 1)
                        if is_later(k, 2):
                            pool.wait_ge(v_mm, k - 1)
                        nc.gpsimd.tensor_tensor(gl[:, u, :], gauss[:, u, :], g_upper[:, u, :], ALU.subtract).then_inc(gl_ok, 1)
                all_groups(pool, step)

            @block.scalar
            def _(act):
                def step(b, s, live):
                    if live(LN):
                        j, u = back(b, s, LN)[2], (s - LN) % 2
                        act.wait_ge(cap_ok, j + 1)
                        nc.scalar.activation(ex[:, u, :], ex[:, u, :], ACT.Ln, scale=0.5, bias=0.5).then_inc(ln_ok, 1)
                    if live(GAUSS):
                        k, v = back(b, s, GAUSS)[2], (s - GAUSS) % 2
                        act.wait_ge(e_mm, k + 1)
                        nc.scalar.activation(dist2[:, v, :], ps_e[:, :], ACT.Square, bias=col[:, C_NOFF:C_NOFF + 1]).then_inc(sq_ok, 1)
                    if live(FIRST):
                        j, u = back(b, s, FIRST)[2], (s - FIRST) % 2
                        act.wait_ge(v_mm, j + 1)
                        if is_later(j, 2):
                            act.wait_ge(h_ok, j - 1)
                        nc.scalar.activation(ex[:, u, :], ps_v[:, u, :], ACT.Exp, bias=col[:, C_B1:C_B1 + 1]).then_inc(ev_ok, 1)
                    if live(GAUSS):
                        act.wait_ge(sq_ok, k + 1)
                        if is_later(k, 2):
                            act.wait_ge(v_mm, k - 1)
                        nc.scalar.activation(gauss[:, v, :], dist2[:, v, :], ACT.Exp, scale=coeff).then_inc(g_ok, 1)
                nc.scalar.preload_act_table_set("natural_log_exp_and_others")
                all_groups(act, step)

            @block.vector
            def _(dve):
                def evacuate(b, side):
                    dve.wait_ge(y_mm, b * GPB + (side + 1) * HG)
                    start = b * P + side * HG * ROWS
                    y = y_all[:, start:start + HG * ROWS] if isinstance(start, int) else y_all[:, bass.ds(start, HG * ROWS)]
                    y2 = ps_y[:, 0:2 * HG * ROWS].rearrange("p (c t) -> p t c", t=2)
                    nc.vector.tensor_tensor(y, y2[:, 0, :], y, ALU.add).then_inc(y_half, 1)
                    dve.wait_ge(y_half, 2 * b + side + 1)
                    nc.vector.tensor_tensor(y, y2[:, 1, :], y, ALU.add).then_inc(y_ev, 1)

                def fetch_a2(b, side):
                    start = b * P + side * HG * ROWS
                    src = adj_t[:, start:start + HG * ROWS] if isinstance(start, int) else adj_t[:, bass.ds(start, HG * ROWS)]
                    nc.vector.tensor_copy(a2_half[:, :], src).then_inc(a2_in, 1)

                def weigh(b, s, k, side):
                    u = s % 2
                    rf = at(rf_all, b).unsqueeze(1).to_broadcast([P, HALF, P])
                    dve.wait_ge(w_mm, 2 * k + 1 + side)
                    if side == 0 and is_later(k, 2):
                        dve.wait_ge(y_mm, k - 1)
                        dve.wait_ge(zl_ok, k - 1)
                    nc.vector.tensor_tensor(zt[:, u, side * 512:(side + 1) * 512].rearrange("p (i f) -> p i f", f=P),
                                            ps_w[:, side, :].rearrange("p (i f) -> p i f", f=P), rf, ALU.mult).then_inc(z_ok, 1)

                def step(b, s, live):
                    if s == GATHER:
                        if is_later(b, 1):
                            evacuate(b - 1, 1)
                        fetch_a2(b, 0)
                    if s == GATHER + HG:
                        evacuate(b, 0)
                        fetch_a2(b, 1)
                    if live(LN):
                        j, u = back(b, s, LN)[2], (s - LN) % 2
                        dve.wait_ge(ln_ok, j + 1)
                        if is_later(j, 2):
                            dve.wait_ge(w_mm, 2 * (j - 1))
                        nc.vector.scalar_tensor_tensor(h[:, u, :], ps_v[:, u, :], b1_ln2[:, 0:1], ex[:, u, :],
                                                       ALU.add, ALU.max).then_inc(h_ok, 1)
                    if live(SECOND):
                        weigh(*back(b, s, SECOND), 0)
                    if live(FIRST):
                        j, u = back(b, s, FIRST)[2], (s - FIRST) % 2
                        dve.wait_ge(ev_ok, j + 1)
                        nc.vector.tensor_scalar_min(ex[:, u, :], ex[:, u, :], EXP_CAP).then_inc(cap_ok, 1)
                    if live(SECOND):
                        weigh(*back(b, s, SECOND), 1)
                all_groups(dve, step)
                evacuate(B - 1, 1)

        Q = 4
        with ExitStack() as cx, nc.Block() as block:
            def tmp(name, shape, dt=F32):
                return cx.enter_context(nc.sbuf_tensor("l3e_" + name, shape, dt))

            def ps(name):
                return cx.enter_context(nc.psum_tensor("l3e_" + name, [P, 2, 512], F32))

            ex, s, t_o = (tmp(n, [P, 2, Q * P]) for n in ("ex", "s", "t"))
            ps_d, ps_o = ps("ps_d"), ps("ps_o")
            d_mm, ev_ok, cap_ok, ln_ok, s_ok, o_mm, t_ok, r_ok = (
                cx.enter_context(nc.semaphore("l3e_" + n))
                for n in ("d_mm", "ev_ok", "cap_ok", "ln_ok", "s_ok", "o_mm", "t_ok", "r_ok"))

            @block.tensor
            def _(pe):
                for c in range(B // Q):
                    u = c % 2
                    if c >= 2:
                        pe.wait_ge(s_ok, c - 1)
                    nc.tensor.matmul(ps_d[:, u, :], wt[:, WD1T, :], y_all[:, c * Q * P:(c + 1) * Q * P], start=True, stop=True).then_inc(d_mm, 1)
                    pe.wait_ge(s_ok, c + 1)
                    if c >= 2:
                        pe.wait_ge(t_ok, c - 1)
                    for q in range(Q):
                        last = nc.tensor.matmul(ps_o[:, u, q * P:(q + 1) * P], s[:, u, q * P:(q + 1) * P], wt[:, WD2T, :],
                                                start=True, stop=True)
                    last.then_inc(o_mm, 1)

            @block.scalar
            def _(act):
                for c in range(B // Q):
                    u = c % 2
                    act.wait_ge(d_mm, c + 1)
                    if c >= 2:
                        act.wait_ge(s_ok, c - 1)
                    nc.scalar.activation(ex[:, u, :], ps_d[:, u, :], ACT.Exp, bias=col[:, C_BD1:C_BD1 + 1]).then_inc(ev_ok, 1)
                    act.wait_ge(cap_ok, c + 1)
                    nc.scalar.activation(ex[:, u, :], ex[:, u, :], ACT.Ln, scale=0.5, bias=0.5).then_inc(ln_ok, 1)

            @block.vector
            def _(dve):
                for c in range(B // Q):
                    u = c % 2
                    dve.wait_ge(ev_ok, c + 1)
                    nc.vector.tensor_scalar_min(ex[:, u, :], ex[:, u, :], EXP_CAP).then_inc(cap_ok, 1)
                    dve.wait_ge(ln_ok, c + 1)
                    if c >= 2:
                        dve.wait_ge(o_mm, c - 1)
                    nc.vector.scalar_tensor_tensor(s[:, u, :], ps_d[:, u, :], bd1_ln2[:, 0:1], ex[:, u, :],
                                                   ALU.add, ALU.max).then_inc(s_ok, 1)
                    dve.wait_ge(o_mm, c + 1)
                    chunk = x_all[:, c * Q * P:(c + 1) * Q * P].rearrange("p (q e) -> p q e", e=P)
                    to3 = t_o[:, u, :].rearrange("p (q e) -> p q e", e=P)
                    nc.vector.tensor_tensor(to3, ps_o[:, u, :].rearrange("p (q e) -> p q e", e=P),
                                            row[:, R_BD2, :].unsqueeze(1).to_broadcast([P, Q, P]), ALU.add).then_inc(t_ok, 1)
                    dve.wait_ge(t_ok, c + 1)
                    nc.vector.tensor_tensor(chunk, to3, chunk, ALU.add).then_inc(r_ok, 1)
                    dve.wait_ge(r_ok, c + 1)
                    for q in range(Q):
                        row_stats(c * Q + q)

        rstd_phase("ln3")

        with ExitStack() as cx, nc.Block() as block:
            n_ok = cx.enter_context(nc.semaphore("out_n_ok"))
            stored = cx.enter_context(nc.semaphore("stored"))

            @block.vector
            def _(dve):
                with dve.Fori(0, B) as b:
                    normalise(at(x_all, b), at(x_all, b), b).then_inc(n_ok, 1)

            @block.sync
            def _(sp):
                for c in range(B // Q):
                    sp.wait_ge(n_ok, (c + 1) * Q)
                    sp.dma_start(out[c * Q:(c + 1) * Q].rearrange("b n d -> n b d"),
                                 x_all[:, c * Q * P:(c + 1) * Q * P].rearrange("p (b d) -> p b d", d=P)).then_inc(stored, 16)
                sp.wait_ge(stored, 16 * (B // Q))


def kernel(**inputs):
    import numpy as _np
    import concourse.bacc as _bacc
    from concourse import mybir as _mybir
    from concourse.bass_utils import run_bass_kernel_spmd as _run

    g = {n: _np.asarray(a) for n, a in inputs.items()}
    n_graphs = g["x"].shape[0]
    eye = _np.eye(P, dtype=_np.float32)
    off = _np.linspace(0.0, CUTOFF, NG, dtype=_np.float32)
    neg_offsets = _np.concatenate([-off, -off])
    side_of_row = _np.tile(_np.repeat(_np.eye(2, dtype=_np.float32), P // 2, axis=1), (3, 1))
    l1 = {n[len("L1_gnn_"):]: a for n, a in g.items() if n.startswith("L1_gnn_")}
    l3 = {n[len("L3_gnn_"):]: a for n, a in g.items() if n.startswith("L3_gnn_")}
    host = {
        "x": g["x"],
        "adj": g["adj"],
        "adjt": g["adj"].transpose(0, 2, 1),
        "weights": _np.stack([g["L0_gnn_W"].T, l1["W_ir"], l1["W_iz"], l1["W_im"], l1["W_xr"], l1["W_xz"], l1["W_xm"],
                              l1["W_hr"], l1["W_hz"], l1["W_hm"], g["L2_gnn_theta"], l3["Wa"].T, l3["W2"].T,
                              l3["Wd1"].T, l3["Wd2"].T, eye, 1 - eye], axis=1),
        "w1t": l3["W1"].T,
        "columns": _np.stack([l1["b_xr"], l1["b_hr"], l1["b_xz"], l1["b_hz"], l1["b_xm"], l1["b_hm"],
                              l3["b1"], l3["b2"], l3["bd1"], neg_offsets], axis=1),
        "rows": _np.stack([g["L0_gnn_b"], l1["b_ir"], l1["b_iz"], l1["b_im"], g["L2_gnn_bias"], l3["bd2"]], axis=0),
        "halves": side_of_row,
    }
    nc = _bacc.Bacc("TRN2", target_bir_lowering=False, num_devices=1)
    arrays, args = {}, []
    for name, a in host.items():
        a = _np.ascontiguousarray(a)
        arrays[f"in_{name}_dram"] = a
        args.append(nc.dram_tensor(f"in_{name}_dram", a.shape, _mybir.dt.from_np(a.dtype), kind="ExternalInput").ap())
    out = nc.dram_tensor("out_dram", g["x"].shape, _mybir.dt.float32, kind="ExternalOutput").ap()
    parts = nc.dram_tensor("adj_parts_dram", (3, n_graphs, P, P), _mybir.dt.bfloat16).ap()
    build(nc, n_graphs, *args, out, parts)
    r = _run(nc, [arrays], core_ids=[0])
    return r.results[0]["out_dram"]
```

```python
from contextlib import ExitStack

import numpy as np

import concourse.bass as bass
from concourse import mybir

ALU = mybir.AluOpType
ACT = mybir.ActivationFunctionType
F32 = mybir.dt.float32
BF16 = mybir.dt.bfloat16

P = 128
NG = 64
CUTOFF = 5.0
LN2 = float(np.log(2.0))
LN_EPS = 1e-5
DEG_EPS = 1e-6
EXP_CAP = 2.0 ** 60

(W0T, WIR, WIZ, WIM, WXR, WXZ, WXM, WHR, WHZ, WHM, THETA, WAT, W2T, WD1T, WD2T, IDENT, OFFD) = range(17)
(C_XR, C_HR, C_XZ, C_HZ, C_XM, C_HM, C_B1, C_B2, C_BD1, C_NOFF) = range(10)
(R_B0, R_IR, R_IZ, R_IM, R_BIAS2, R_BD2) = range(6)

ROWS = 8
HALF = ROWS // 2
GPB = P // ROWS


def is_later(k, d):
    return k >= d if isinstance(k, int) else True


def run_steps(eng, total, lags, body):
    for k in range(min(4, total)):
        body(k, k % 2, lambda lag: k - lag >= 0)
    if total > 4:
        with eng.Fori(2, total // 2) as i:
            for u in range(2):
                body(2 * i + u, u, lambda lag: True)
    for k in range(total, total + lags):
        body(k, k % 2, lambda lag: 0 <= k - lag < total)


def build(nc, B, x, adj, adjt, weights, w1t, columns, rows, halves, out, parts):
    offsets = np.linspace(0.0, CUTOFF, NG, dtype=np.float32)
    width = offsets[1] - offsets[0]
    coeff = float(np.float32(-0.5) / (width * width))

    ctx = ExitStack()
    with ctx:
        def sb(name, shape, dt=F32):
            return ctx.enter_context(nc.sbuf_tensor(name, shape, dt))

        def sem(name):
            return ctx.enter_context(nc.semaphore(name))

        x_all = sb("x_all", [P, B * P])
        adj_t = sb("adj_t", [P, B * P])
        big = sb("big", [P, 3 * B * P])
        wt = sb("wt", [P, 17, P])
        w1 = sb("w1", [P, P])
        w1_hi = sb("w1_hi", [P, P], BF16)
        w1_lo = sb("w1_lo", [P, P], BF16)
        col = sb("col", [P, 10])
        row = sb("row", [P, 6, P])
        half_f = sb("half_f", [6, P])
        half = sb("half", [6, P], BF16)
        b_gate = sb("b_gate", [P, 2])
        b1_ln2 = sb("b1_ln2", [P, 1])
        bd1_ln2 = sb("bd1_ln2", [P, 1])
        deg = sb("deg", [P, 2, B])
        root = sb("root", [P, 2, B])
        dinv = sb("dinv", [P, 2, B])
        mean = sb("mean", [P, B])
        part_sq = sb("part_sq", [P, 2, B])
        var_eps = sb("var_eps", [P, B])
        std = sb("std", [P, B])
        rstd = sb("rstd", [P, B])
        six = sb("six", [P, B, 6])

        ident = wt[:, IDENT, :]

        def at(t, b):
            return t[:, b * P:(b + 1) * P] if isinstance(b, int) else t[:, bass.ds(b * P, P)]

        def duo(t, g):
            return t[:, g * 2 * P:(g + 1) * 2 * P] if isinstance(g, int) else t[:, bass.ds(g * (2 * P), 2 * P)]

        def columns2(t, g):
            return t[:, 2 * g:2 * g + 2] if isinstance(g, int) else t[:, bass.ds(g * 2, 2)]

        def apart(t):
            return t.rearrange("p (q c) -> p q c", q=2)

        def twice(t):
            return t.unsqueeze(1).to_broadcast([P, 2, P])

        PAIRS = B // 2
        QS = [(q, slice(q * P, (q + 1) * P)) for q in range(2)]

        def column(t, b):
            return t[:, b:b + 1] if isinstance(b, int) else t[:, bass.ds(b, 1)]

        with ExitStack() as cx, nc.Block() as block:
            s_w, s_x = (cx.enter_context(nc.semaphore(n)) for n in ("ld_w", "ld_x"))
            LOADS = 4
            s_at = [cx.enter_context(nc.semaphore(f"ld_adj_t{c}")) for c in range(LOADS)]
            deg_sum = cx.enter_context(nc.semaphore("deg_sum"))
            deg_sh = cx.enter_context(nc.semaphore("deg_shifted"))
            root_ok = cx.enter_context(nc.semaphore("root_ok"))
            w1_hi_ok = cx.enter_context(nc.semaphore("w1_hi_ok"))
            ones_ok = cx.enter_context(nc.semaphore("ones_ok"))
            ones = cx.enter_context(nc.sbuf_tensor("ld_ones", [P, 1], F32))
            ps_deg = cx.enter_context(nc.psum_tensor("ld_ps_deg", [P, 512], F32))

            @block.sync
            def _(sp):
                for c in range(LOADS):
                    g = slice(c * B // LOADS, (c + 1) * B // LOADS)
                    sp.dma_start(adj_t[:, g.start * P:g.stop * P].rearrange("p (b j) -> p b j", j=P),
                                 adjt[g].rearrange("b i j -> i b j")).then_inc(s_at[c], 16)
                sp.dma_start(x_all[:, :].rearrange("p (b j) -> p b j", j=P), x.rearrange("b i j -> i b j")).then_inc(s_x, 16)
                sp.wait_ge(s_x, 16)
                for c in range(LOADS):
                    sp.wait_ge(s_at[c], 16)

            @block.scalar
            def _(act):
                act.dma_start(wt[:, :, :], weights).then_inc(s_w, 16)
                act.dma_start(w1[0:NG, :], w1t).then_inc(s_w, 16)
                act.dma_start(w1[NG:P, :], w1t).then_inc(s_w, 16)
                act.dma_start(col[:, :], columns).then_inc(s_w, 16)
                act.dma_start(row[:, :, :], rows.partition_broadcast(P)).then_inc(s_w, 16)
                act.dma_start(half_f[:, :], halves).then_inc(s_w, 16)
                act.wait_ge(deg_sh, 2)
                nc.scalar.activation(root[:, :, :], deg[:, :, :], ACT.Sqrt).then_inc(root_ok, 1)

            @block.tensor
            def _(pe):
                pe.wait_ge(ones_ok, 1)
                for b in range(B):
                    if b % (B // LOADS) == 0:
                        pe.wait_ge(s_at[b * LOADS // B], 16)
                    last = nc.tensor.matmul(ps_deg[:, b:b + 1], at(adj_t, b), ones[:, :], start=True, stop=True)
                last.then_inc(deg_sum, 1)

            @block.vector
            def _(dve):
                nc.vector.memset(ones[:, :], 1.0).then_inc(ones_ok, 1)
                dve.wait_ge(deg_sum, 1)
                nc.vector.tensor_scalar_add(deg[:, 1, :], ps_deg[:, 0:B], 1.0).then_inc(deg_sh, 1)
                dve.wait_ge(deg_sh, 1)
                nc.vector.tensor_scalar_add(deg[:, 0, :], deg[:, 1, :], DEG_EPS).then_inc(deg_sh, 1)
                dve.wait_ge(s_w, 96)
                nc.vector.tensor_copy(half[:, :], half_f[:, :])
                nc.vector.tensor_copy(w1_hi[:, :], w1[:, :]).then_inc(w1_hi_ok, 1)
                dve.wait_ge(w1_hi_ok, 1)
                nc.vector.tensor_tensor(w1_lo[:, :], w1[:, :], w1_hi[:, :], ALU.subtract)
                nc.vector.tensor_tensor(b_gate[:, 0:1], col[:, C_XR:C_XR + 1], col[:, C_HR:C_HR + 1], ALU.add)
                nc.vector.tensor_tensor(b_gate[:, 1:2], col[:, C_XZ:C_XZ + 1], col[:, C_HZ:C_HZ + 1], ALU.add)
                nc.vector.tensor_scalar_add(b1_ln2[:, :], col[:, C_B1:C_B1 + 1], -LN2)
                nc.vector.tensor_scalar_add(bd1_ln2[:, :], col[:, C_BD1:C_BD1 + 1], -LN2)
                dve.wait_ge(root_ok, 1)
                nc.vector.reciprocal(dinv[:, :, :], root[:, :, :])

        def rstd_phase(name):
            with ExitStack() as cx, nc.Block() as block:
                step = cx.enter_context(nc.semaphore(name + "_step"))
                ve_ok = cx.enter_context(nc.semaphore(name + "_var_eps"))
                std_ok = cx.enter_context(nc.semaphore(name + "_std"))

                @block.vector
                def _(dve):
                    nc.vector.tensor_tensor(mean[:, :], six[:, :, 1], six[:, :, 4], ALU.add).then_inc(step, 1)
                    nc.vector.tensor_tensor(part_sq[:, 0, :], six[:, :, 1], six[:, :, 4], ALU.subtract).then_inc(step, 1)
                    nc.vector.tensor_tensor(var_eps[:, :], six[:, :, 2], six[:, :, 5], ALU.add).then_inc(step, 1)
                    dve.wait_ge(step, 3)
                    nc.vector.tensor_scalar(mean[:, :], mean[:, :], 0.5, None, ALU.mult)
                    nc.vector.tensor_tensor(part_sq[:, 1, :], part_sq[:, 0, :], part_sq[:, 0, :], ALU.mult).then_inc(step, 1)
                    nc.vector.tensor_scalar(var_eps[:, :], var_eps[:, :], 1.0 / P, LN_EPS, ALU.mult, ALU.add).then_inc(step, 1)
                    dve.wait_ge(step, 5)
                    nc.vector.scalar_tensor_tensor(var_eps[:, :], part_sq[:, 1, :], 0.25, var_eps[:, :], ALU.mult, ALU.add).then_inc(ve_ok, 1)
                    dve.wait_ge(std_ok, 1)
                    nc.vector.reciprocal(rstd[:, :], std[:, :])

                @block.scalar
                def _(act):
                    act.wait_ge(ve_ok, 1)
                    nc.scalar.activation(std[:, :], var_eps[:, :], ACT.Sqrt).then_inc(std_ok, 1)

        def normalise(dst, src, b):
            return nc.vector.tensor_scalar(dst, src, column(mean, b),
                                           column(rstd, b), ALU.subtract, ALU.mult)

        def normalise2(dst, g):
            src, m, rs = duo(x_all, g), columns2(mean, g), columns2(rstd, g)
            for q, c in QS:
                last = nc.vector.tensor_scalar(dst[:, c], src[:, c], m[:, q:q + 1], rs[:, q:q + 1], ALU.subtract, ALU.mult)
            return last

        def row_stats2(g):
            dst = six[:, 2 * g:2 * g + 2, :] if isinstance(g, int) else six[:, bass.ds(g * 2, 2), :]
            src = duo(x_all, g)
            for q, c in QS:
                nc.vector.bn_stats(dst[:, q, :], src[:, c])

        def row_stats(b):
            dst = six[:, b, :] if isinstance(b, int) else six[:, bass.ds(b, 1), :].rearrange("p a c -> p (a c)")
            nc.vector.bn_stats(dst, at(x_all, b))

        with ExitStack() as cx, nc.Block() as block:
            def tmp(name, shape, dt=F32):
                return cx.enter_context(nc.sbuf_tensor("l0_" + name, shape, dt))

            def ps(name):
                return cx.enter_context(nc.psum_tensor("l0_" + name, [P, 2, 512], F32))

            ah, xs, st, t_o = (tmp(n, [P, 2, 2 * P]) for n in ("ah", "xs", "st", "t"))
            ps_s, ps_o = ps("ps_s"), ps("ps_o")
            ah_ok, xs_ok, s_ok, st_ok, o_ok, t_ok, r_ok = (
                cx.enter_context(nc.semaphore("l0_" + n))
                for n in ("ah_ok", "xs_ok", "s_ok", "st_ok", "o_ok", "t_ok", "r_ok"))

            @block.gpsimd
            def _(pool):
                def body(g, u, live):
                    if is_later(g, 2):
                        pool.wait_ge(s_ok, g - 1)
                    nc.gpsimd.tensor_tensor(apart(ah[:, u, :]), apart(duo(adj_t, g)), twice(ident), ALU.add).then_inc(ah_ok, 1)
                run_steps(pool, PAIRS, 0, body)

            @block.tensor
            def _(pe):
                def body(g, u, live):
                    if live(0):
                        pe.wait_ge(ah_ok, g + 1)
                        pe.wait_ge(xs_ok, g + 1)
                        if is_later(g, 2):
                            pe.wait_ge(st_ok, g - 1)
                        for q, c in QS:
                            last = nc.tensor.matmul(ps_s[:, u, c], xs[:, u, c], ah[:, u, c], start=True, stop=True)
                        last.then_inc(s_ok, 1)
                    if live(1):
                        j, v = g - 1, 1 - u
                        pe.wait_ge(st_ok, j + 1)
                        if is_later(j, 2):
                            pe.wait_ge(t_ok, j - 1)
                        for q, c in QS:
                            last = nc.tensor.matmul(ps_o[:, v, c], st[:, v, c], wt[:, W0T, :], start=True, stop=True)
                        last.then_inc(o_ok, 1)
                run_steps(pe, PAIRS, 1, body)

            @block.scalar
            def _(act):
                def body(g, u, live):
                    if live(0):
                        x2, d = duo(x_all, g), columns2(dinv[:, 0, :], g)
                        if is_later(g, 2):
                            act.wait_ge(s_ok, g - 1)
                        for q, c in QS:
                            last = nc.scalar.activation(xs[:, u, c], x2[:, c], ACT.Copy, scale=d[:, q:q + 1])
                        last.then_inc(xs_ok, 1)
                    if live(1):
                        j, v = g - 1, 1 - u
                        act.wait_ge(s_ok, j + 1)
                        if is_later(j, 2):
                            act.wait_ge(o_ok, j - 1)
                        nc.scalar.copy(st[:, v, :], ps_s[:, v, 0:2 * P]).then_inc(st_ok, 1)
                run_steps(act, PAIRS, 1, body)

            @block.vector
            def _(dve):
                def body(g, u, live):
                    if live(2):
                        j = g - 2
                        d = columns2(dinv[:, 0, :], j)
                        dve.wait_ge(o_ok, j + 1)
                        for q, c in QS:
                            last = nc.vector.scalar_tensor_tensor(t_o[:, u, c], ps_o[:, u, c], d[:, q:q + 1], row[:, R_B0, :],
                                                                  ALU.mult, ALU.add)
                        last.then_inc(t_ok, 1)
                    if live(3):
                        dve.wait_ge(r_ok, g - 2)
                        row_stats2(g - 3)
                    if live(2):
                        dve.wait_ge(t_ok, j + 1)
                        nc.vector.scalar_tensor_tensor(duo(x_all, j), t_o[:, u, :], 0.0, duo(x_all, j), ALU.max, ALU.add).then_inc(r_ok, 1)
                run_steps(dve, PAIRS, 3, body)

        rstd_phase("ln0")

        gates = big[:, :].rearrange("p (t c b) -> p t c b", c=3, b=B)
        with ExitStack() as cx, nc.Block() as block:
            def tmp(name, shape, dt=F32):
                return cx.enter_context(nc.sbuf_tensor("l1_" + name, shape, dt))

            def ps(name):
                return cx.enter_context(nc.psum_tensor("l1_" + name, [P, 2, 512], F32))

            x1, x1t, gt = (tmp(n, [P, 2, 2 * P]) for n in ("x1", "x1t", "gt"))
            proj = tmp("proj", [P, 2, 2, 3 * P])
            ps_t, ps_p = ps("ps_t"), ps("ps_p")
            ps_a = cx.enter_context(nc.psum_tensor("l1_ps_a", [P, 2, 2, 512], F32))
            n_ok, cp_ok, g_ok, t_ok, xt_ok, p_ok, pj_ok, a_ok, ev_ok = (
                cx.enter_context(nc.semaphore("l1_" + n))
                for n in ("n_ok", "cp_ok", "g_ok", "t_ok", "xt_ok", "p_ok", "pj_ok", "a_ok", "ev_ok"))

            @block.gpsimd
            def _(pool):
                def body(g, u, live):
                    if is_later(g, 2):
                        pool.wait_ge(a_ok, g - 1)
                    pool.wait_ge(n_ok, g + 1)
                    nc.gpsimd.tensor_tensor(apart(gt[:, u, :]), apart(duo(adj_t, g)), twice(wt[:, OFFD, :]), ALU.mult).then_inc(g_ok, 1)
                    nc.gpsimd.tensor_copy(duo(x_all, g), x1[:, u, :]).then_inc(cp_ok, 1)
                run_steps(pool, PAIRS, 0, body)

            @block.vector
            def _(dve):
                def body(g, u, live):
                    if live(0):
                        if is_later(g, 2):
                            dve.wait_ge(t_ok, g - 1)
                            dve.wait_ge(cp_ok, g - 1)
                        normalise2(x1[:, u, :], g).then_inc(n_ok, 1)
                    if live(1):
                        j, v = g - 1, 1 - u
                        if is_later(j, 2):
                            dve.wait_ge(a_ok, j - 1)
                        for q in range(2):
                            dve.wait_ge(p_ok, 2 * j + 1 + q)
                            nc.vector.tensor_tensor(proj[:, v, q, :], ps_p[:, q, 0:3 * P],
                                                    row[:, R_IR:R_IM + 1, :].rearrange("p a b -> p (a b)"), ALU.add).then_inc(pj_ok, 1)
                run_steps(dve, PAIRS, 1, body)

            @block.tensor
            def _(pe):
                def body(g, u, live):
                    if live(1):
                        j, v = g - 1, 1 - u
                        pe.wait_ge(xt_ok, j + 1)
                        for q, c in QS:
                            if is_later(j, 1):
                                pe.wait_ge(pj_ok, 2 * j - 1 + q)
                            nc.tensor.matmul(ps_p[:, q, 0:3 * P], x1t[:, v, c], wt[:, WIR:WIM + 1, :].rearrange("p a b -> p (a b)"),
                                             start=True, stop=True).then_inc(p_ok, 1)
                    if live(0):
                        pe.wait_ge(n_ok, g + 1)
                        if is_later(g, 2):
                            pe.wait_ge(xt_ok, g - 1)
                        for q, c in QS:
                            last = nc.tensor.transpose(ps_t[:, u, c], x1[:, u, c], ident)
                        last.then_inc(t_ok, 1)
                    if live(2):
                        j = g - 2
                        pe.wait_ge(pj_ok, 2 * j + 2)
                        pe.wait_ge(g_ok, j + 1)
                        if is_later(j, 2):
                            pe.wait_ge(ev_ok, 3 * (j - 1))
                        for q, c in QS:
                            for a in range(3):
                                nc.tensor.matmul(ps_a[:, u, q, a * P:(a + 1) * P], wt[:, WXR + a, :], x1t[:, u, c], start=True, stop=False)
                                last = nc.tensor.matmul(ps_a[:, u, q, a * P:(a + 1) * P], proj[:, u, q, a * P:(a + 1) * P], gt[:, u, c],
                                                        start=False, stop=True)
                        last.then_inc(a_ok, 1)
                run_steps(pe, PAIRS, 2, body)

            @block.scalar
            def _(act):
                def body(g, u, live):
                    if live(3):
                        j, v = g - 3, 1 - u
                        act.wait_ge(a_ok, j + 1)
                        for a, bias in enumerate((b_gate[:, 0:1], b_gate[:, 1:2], col[:, C_XM:C_XM + 1])):
                            dst = gates[:, :, a, 2 * j:2 * j + 2] if isinstance(j, int) else gates[:, :, a, bass.ds(2 * j, 2)]
                            nc.scalar.activation(dst.rearrange("p t q -> p q t"), ps_a[:, v, :, a * P:(a + 1) * P],
                                                 ACT.Identity, bias=bias).then_inc(ev_ok, 1)
                    if live(0):
                        act.wait_ge(t_ok, g + 1)
                        if is_later(g, 2):
                            act.wait_ge(a_ok, g - 1)
                        nc.scalar.copy(x1t[:, u, :], ps_t[:, u, 0:2 * P]).then_inc(xt_ok, 1)
                run_steps(act, PAIRS, 3, body)

        with ExitStack() as cx, nc.Block() as block:
            def tmp(name, shape, dt=F32):
                return cx.enter_context(nc.sbuf_tensor("gru_" + name, shape, dt))

            def ps(name):
                return cx.enter_context(nc.psum_tensor("gru_" + name, [P, 2, 512], F32))

            r, z, m, t1, t2, omz, zh, om = (tmp(n, [P, 2, B]) for n in ("r", "z", "m", "t1", "t2", "omz", "zh", "om"))
            h, g_m = (tmp(n, [P, 2, B]) for n in ("h", "g_m"))
            CUT = 2
            an = tmp("an", [P, 2, CUT * P])
            rest = tmp("rest", [P, 2, CUT * P])
            cut = tmp("cut", [P, 2, 3, CUT * P], BF16)
            ps_r, ps_z, ps_m = ps("ps_r"), ps("ps_z"), ps("ps_m")
            (init_ok, r_mm, m_mm, z_mm, r_s, z_s, m_s, t1_ok, t2_ok, from_z, om_ok, h_ok) = (
                cx.enter_context(nc.semaphore("gru_" + n))
                for n in ("init", "r_mm", "m_mm", "z_mm", "r_s", "z_s", "m_s", "t1_ok", "t2_ok", "from_z", "om_ok", "h_ok"))
            kept, gm_ok = (cx.enter_context(nc.semaphore("gru_" + n)) for n in ("kept", "gm_ok"))
            an_in = [cx.enter_context(nc.semaphore(f"cut_in{u}")) for u in range(2)]
            cut_out = [cx.enter_context(nc.semaphore(f"cut_out{u}")) for u in range(2)]
            cut_step = cx.enter_context(nc.semaphore("cut_step"))

            def gate(eng, t, c):
                if isinstance(t, int):
                    return gates[:, t, c, :]
                return big[:, bass.ds(eng.snap(t * (3 * B) + c * B), B)]

            @block.vector
            def _(dve):
                nc.vector.memset(h[:, 1, :], 0.0).then_inc(init_ok, 1)
                dve.wait_ge(init_ok, 1)

                def body(t, u, live):
                    both = 2 * t + 2 if isinstance(t, int) else dve.snap(2 * t + 2)
                    if is_later(t, 2):
                        dve.wait_ge(kept, t - 1)
                    dve.wait_ge(r_s, t + 1)
                    dve.wait_ge(m_mm, t + 1)
                    nc.vector.scalar_tensor_tensor(t1[:, u, :], ps_m[:, u, 0:B], col[:, C_HM:C_HM + 1], r[:, u, :],
                                                   ALU.add, ALU.mult).then_inc(t1_ok, 1)
                    dve.wait_ge(gm_ok, t + 1)
                    dve.wait_ge(t1_ok, t + 1)
                    nc.vector.tensor_tensor(t2[:, u, :], t1[:, u, :], g_m[:, u, :], ALU.add).then_inc(t2_ok, 1)
                    dve.wait_ge(z_s, t + 1)
                    nc.vector.tensor_scalar(omz[:, u, :], z[:, u, :], -1.0, 1.0, ALU.mult, ALU.add).then_inc(from_z, 1)
                    nc.vector.tensor_tensor(zh[:, u, :], z[:, u, :], h[:, 1 - u, :], ALU.mult).then_inc(from_z, 1)
                    dve.wait_ge(from_z, both)
                    dve.wait_ge(m_s, t + 1)
                    nc.vector.tensor_tensor(om[:, u, :], omz[:, u, :], m[:, u, :], ALU.mult).then_inc(om_ok, 1)
                    dve.wait_ge(om_ok, t + 1)
                    nc.vector.tensor_tensor(h[:, u, :], om[:, u, :], zh[:, u, :], ALU.add).then_inc(h_ok, 1)
                run_steps(dve, P, 0, body)

            @block.scalar
            def _(act):
                def keep(t, u):
                    dst = gate(act, t, 0)
                    act.wait_ge(h_ok, t + 1)
                    nc.scalar.copy(dst, h[:, u, :]).then_inc(kept, 1)

                def body(t, u, live):
                    act.wait_ge(r_mm, t + 1)
                    nc.scalar.activation(r[:, u, :], ps_r[:, u, 0:B], ACT.Sigmoid).then_inc(r_s, 1)
                    if is_later(t, 2):
                        act.wait_ge(t2_ok, t - 1)
                    nc.scalar.copy(g_m[:, u, :], gate(act, t, 2)).then_inc(gm_ok, 1)
                    if is_later(t, 1):
                        keep(t - 1, 1 - u)
                    act.wait_ge(z_mm, t + 1)
                    nc.scalar.activation(z[:, u, :], ps_z[:, u, 0:B], ACT.Sigmoid).then_inc(z_s, 1)
                    act.wait_ge(t2_ok, t + 1)
                    nc.scalar.activation(m[:, u, :], t2[:, u, :], ACT.Tanh).then_inc(m_s, 1)
                nc.scalar.preload_act_table_set("sigmoid_and_others")
                run_steps(act, P, 0, body)
                keep(P - 1, (P - 1) % 2)

            @block.tensor
            def _(pe):
                def seed(t, u):
                    for c, dst in enumerate((ps_r, ps_z)):
                        nc.tensor.matmul(dst[:, u, 0:B], ident, gate(pe, t, c), start=True, stop=False)

                seed(0, 0)
                pe.wait_ge(init_ok, 1)

                def body(t, u, live):
                    before = h[:, 1 - u, :]
                    if is_later(t, 1):
                        pe.wait_ge(h_ok, t)
                    nc.tensor.matmul(ps_r[:, u, 0:B], wt[:, WHR, :], before, start=False, stop=True).then_inc(r_mm, 1)
                    nc.tensor.matmul(ps_m[:, u, 0:B], wt[:, WHM, :], before, start=True, stop=True).then_inc(m_mm, 1)
                    nc.tensor.matmul(ps_z[:, u, 0:B], wt[:, WHZ, :], before, start=False, stop=True).then_inc(z_mm, 1)
                    if not (isinstance(t, int) and t == P - 1):
                        seed(t + 1, 1 - u)
                for t in range(4):
                    body(t, t % 2, None)
                with pe.Fori(2, P // 2 - 1) as i:
                    for u in range(2):
                        body(2 * i + u, u, None)
                for t in range(P - 2, P):
                    body(t, t % 2, None)

            @block.sync
            def _(sp):
                for c in range(B // CUT + 1):
                    if c < B // CUT:
                        if c >= 2:
                            sp.wait_ge(cut_step, 5 * (c - 1))
                        sp.dma_start(an[:, c % 2, :].rearrange("i (b j) -> i b j", j=P),
                                     adj[c * CUT:(c + 1) * CUT].rearrange("b i j -> i b j")).then_inc(an_in[c % 2], 16)
                    if c >= 1:
                        sp.wait_ge(cut_step, 5 * c)
                        for part in range(3):
                            sp.dma_start(parts[part, (c - 1) * CUT:c * CUT].rearrange("b i j -> i b j"),
                                         cut[:, (c - 1) % 2, part, :].rearrange("i (b j) -> i b j", j=P)).then_inc(cut_out[(c - 1) % 2], 16)
                for u in range(2):
                    sp.wait_ge(cut_out[u], 48 * ((B // CUT + 1 - u) // 2))

            @block.gpsimd
            def _(pool):
                for c in range(B // CUT):
                    u = c % 2
                    pool.wait_ge(an_in[u], 16 * (c // 2 + 1))
                    if c >= 2:
                        pool.wait_ge(cut_out[u], 48 * (c // 2))
                    nc.gpsimd.tensor_copy(cut[:, u, 0, :], an[:, u, :]).then_inc(cut_step, 1)
                    pool.wait_ge(cut_step, 5 * c + 1)
                    nc.gpsimd.tensor_tensor(rest[:, u, :], an[:, u, :], cut[:, u, 0, :], ALU.subtract).then_inc(cut_step, 1)
                    pool.wait_ge(cut_step, 5 * c + 2)
                    nc.gpsimd.tensor_copy(cut[:, u, 1, :], rest[:, u, :]).then_inc(cut_step, 1)
                    pool.wait_ge(cut_step, 5 * c + 3)
                    nc.gpsimd.tensor_tensor(an[:, u, :], rest[:, u, :], cut[:, u, 1, :], ALU.subtract).then_inc(cut_step, 1)
                    pool.wait_ge(cut_step, 5 * c + 4)
                    nc.gpsimd.tensor_copy(cut[:, u, 2, :], an[:, u, :]).then_inc(cut_step, 1)

        with ExitStack() as cx, nc.Block() as block:
            hs = cx.enter_context(nc.sbuf_tensor("l1_hs", [P, 2, 2 * P], F32))
            ps_t = cx.enter_context(nc.psum_tensor("l1_ps_h", [P, 2, 512], F32))
            h_ok, t_ok, r_ok = (cx.enter_context(nc.semaphore("l1s_" + n)) for n in ("h_ok", "t_ok", "r_ok"))

            @block.scalar
            def _(act):
                def body(g, u, live):
                    if is_later(g, 2):
                        act.wait_ge(t_ok, g - 1)
                    src = gates[:, :, 0, 2 * g:2 * g + 2] if isinstance(g, int) else gates[:, :, 0, bass.ds(2 * g, 2)]
                    nc.scalar.activation(apart(hs[:, u, :]), src.rearrange("p t q -> p q t"), ACT.Relu).then_inc(h_ok, 1)
                run_steps(act, PAIRS, 0, body)

            @block.tensor
            def _(pe):
                def body(g, u, live):
                    pe.wait_ge(h_ok, g + 1)
                    if is_later(g, 2):
                        pe.wait_ge(r_ok, g - 1)
                    for q, c in QS:
                        last = nc.tensor.transpose(ps_t[:, u, c], hs[:, u, c], ident)
                    last.then_inc(t_ok, 1)
                run_steps(pe, PAIRS, 0, body)

            @block.vector
            def _(dve):
                def body(g, u, live):
                    if live(0):
                        dve.wait_ge(t_ok, g + 1)
                        nc.vector.tensor_tensor(duo(x_all, g), ps_t[:, u, 0:2 * P], duo(x_all, g), ALU.add).then_inc(r_ok, 1)
                    if live(1):
                        dve.wait_ge(r_ok, g)
                        row_stats2(g - 1)
                run_steps(dve, PAIRS, 1, body)

        rstd_phase("ln1")

        with ExitStack() as cx, nc.Block() as block:
            def tmp(name, shape, dt=F32):
                return cx.enter_context(nc.sbuf_tensor("l2_" + name, shape, dt))

            def ps(name):
                return cx.enter_context(nc.psum_tensor("l2_" + name, [P, 2, 512], F32))

            x2, x2t, ah, sup, t_o = (tmp(n, [P, 2, 2 * P]) for n in ("x2", "x2t", "ah", "sup", "t"))
            ps_t, ps_u, ps_o = ps("ps_t"), ps("ps_u"), ps("ps_o")
            n_ok, cp_ok, ah_ok, t_ok, xt_ok, u_ok, sup_ok, o_ok, to_ok, r_ok = (
                cx.enter_context(nc.semaphore("l2_" + n))
                for n in ("n_ok", "cp_ok", "ah_ok", "t_ok", "xt_ok", "u_ok", "sup_ok", "o_ok", "to_ok", "r_ok"))

            @block.gpsimd
            def _(pool):
                def body(g, u, live):
                    if is_later(g, 2):
                        pool.wait_ge(o_ok, g - 1)
                    pool.wait_ge(n_ok, g + 1)
                    nc.gpsimd.tensor_tensor(apart(ah[:, u, :]), apart(duo(adj_t, g)), twice(ident), ALU.add).then_inc(ah_ok, 1)
                    nc.gpsimd.tensor_copy(duo(x_all, g), x2[:, u, :]).then_inc(cp_ok, 1)
                run_steps(pool, PAIRS, 0, body)

            @block.tensor
            def _(pe):
                def body(g, u, live):
                    if live(0):
                        pe.wait_ge(n_ok, g + 1)
                        if is_later(g, 2):
                            pe.wait_ge(xt_ok, g - 1)
                        for q, c in QS:
                            last = nc.tensor.transpose(ps_t[:, u, c], x2[:, u, c], ident)
                        last.then_inc(t_ok, 1)
                    if live(2):
                        j = g - 2
                        pe.wait_ge(sup_ok, j + 1)
                        pe.wait_ge(ah_ok, j + 1)
                        if is_later(j, 2):
                            pe.wait_ge(to_ok, j - 1)
                        for q, c in QS:
                            last = nc.tensor.matmul(ps_o[:, u, c], ah[:, u, c], sup[:, u, c], start=True, stop=True)
                        last.then_inc(o_ok, 1)
                    if live(1):
                        j, v = g - 1, 1 - u
                        pe.wait_ge(xt_ok, j + 1)
                        if is_later(j, 2):
                            pe.wait_ge(sup_ok, j - 1)
                        for q, c in QS:
                            last = nc.tensor.matmul(ps_u[:, v, c], x2t[:, v, c], wt[:, THETA, :], start=True, stop=True)
                        last.then_inc(u_ok, 1)
                run_steps(pe, PAIRS, 2, body)

            @block.scalar
            def _(act):
                def body(g, u, live):
                    if live(0):
                        act.wait_ge(t_ok, g + 1)
                        if is_later(g, 2):
                            act.wait_ge(u_ok, g - 1)
                        nc.scalar.copy(x2t[:, u, :], ps_t[:, u, 0:2 * P]).then_inc(xt_ok, 1)
                    if live(1):
                        j, v = g - 1, 1 - u
                        d = columns2(dinv[:, 1, :], j)
                        act.wait_ge(u_ok, j + 1)
                        if is_later(j, 2):
                            act.wait_ge(o_ok, j - 1)
                        for q, c in QS:
                            last = nc.scalar.activation(sup[:, v, c], ps_u[:, v, c], ACT.Copy, scale=d[:, q:q + 1])
                        last.then_inc(sup_ok, 1)
                run_steps(act, PAIRS, 1, body)

            @block.vector
            def _(dve):
                def body(g, u, live):
                    if live(0):
                        if is_later(g, 2):
                            dve.wait_ge(t_ok, g - 1)
                            dve.wait_ge(cp_ok, g - 1)
                        normalise2(x2[:, u, :], g).then_inc(n_ok, 1)
                    if live(3):
                        j, v = g - 3, 1 - u
                        d = columns2(dinv[:, 1, :], j)
                        dve.wait_ge(o_ok, j + 1)
                        for q, c in QS:
                            last = nc.vector.scalar_tensor_tensor(t_o[:, v, c], ps_o[:, v, c], d[:, q:q + 1], row[:, R_BIAS2, :],
                                                                  ALU.mult, ALU.add)
                        last.then_inc(to_ok, 1)
                    if live(4):
                        dve.wait_ge(r_ok, g - 3)
                        row_stats2(g - 4)
                    if live(3):
                        dve.wait_ge(to_ok, j + 1)
                        dve.wait_ge(cp_ok, j + 1)
                        nc.vector.tensor_tensor(duo(x_all, j), t_o[:, v, :], duo(x_all, j), ALU.add).then_inc(r_ok, 1)
                run_steps(dve, PAIRS, 4, body)

        rstd_phase("ln2")

        rf_all = big[:, 0:B * P]
        y_all = big[:, B * P:2 * B * P]
        a2_parts = adj_t[:, :].bitcast(BF16)

        def a2_part(g, part):
            return duo(a2_parts.rearrange("p (c t) -> p t c", t=2)[:, part, :], g)

        with ExitStack() as cx, nc.Block() as block:
            def tmp(name, shape, dt=F32):
                return cx.enter_context(nc.sbuf_tensor("l3p_" + name, shape, dt))

            def ps(name):
                return cx.enter_context(nc.psum_tensor("l3p_" + name, [P, 2, 512], F32))

            x3, x3t, rfs, a2 = (tmp(n, [P, 2, 2 * P]) for n in ("x3", "x3t", "rfs", "a2"))
            ps_t, ps_f, ps_q = ps("ps_t"), ps("ps_f"), ps("ps_q")
            n_ok, cp_ok, sq_ok, hi_ok, lo_ok, t_ok, xt_ok, f_ok, rfs_ok, rf_ok, q_ok, y_ok = (
                cx.enter_context(nc.semaphore("l3p_" + n))
                for n in ("n_ok", "cp_ok", "sq_ok", "hi_ok", "lo_ok", "t_ok", "xt_ok", "f_ok", "rfs_ok", "rf_ok", "q_ok", "y_ok"))

            @block.gpsimd
            def _(pool):
                def body(g, u, live):
                    pool.wait_ge(n_ok, g + 1)
                    if is_later(g, 2):
                        pool.wait_ge(q_ok, g - 1)
                        pool.wait_ge(lo_ok, g - 1)
                    nc.gpsimd.tensor_tensor(a2[:, u, :], duo(adj_t, g), duo(adj_t, g), ALU.mult).then_inc(sq_ok, 1)
                    nc.gpsimd.tensor_copy(duo(x_all, g), x3[:, u, :]).then_inc(cp_ok, 1)
                run_steps(pool, PAIRS, 0, body)

            @block.tensor
            def _(pe):
                def body(g, u, live):
                    if live(0):
                        pe.wait_ge(n_ok, g + 1)
                        if is_later(g, 2):
                            pe.wait_ge(xt_ok, g - 1)
                        for q, c in QS:
                            last = nc.tensor.transpose(ps_t[:, u, c], x3[:, u, c], ident)
                        last.then_inc(t_ok, 1)
                    if live(2):
                        j = g - 2
                        pe.wait_ge(rfs_ok, j + 1)
                        pe.wait_ge(sq_ok, j + 1)
                        if is_later(j, 2):
                            pe.wait_ge(y_ok, j - 1)
                        for q, c in QS:
                            last = nc.tensor.matmul(ps_q[:, u, c], rfs[:, u, c], a2[:, u, c], start=True, stop=True)
                        last.then_inc(q_ok, 1)
                    if live(1):
                        j, v = g - 1, 1 - u
                        pe.wait_ge(xt_ok, j + 1)
                        if is_later(j, 2):
                            pe.wait_ge(rfs_ok, j - 1)
                        for q, c in QS:
                            last = nc.tensor.matmul(ps_f[:, v, c], x3t[:, v, c], wt[:, WAT, :], start=True, stop=True)
                        last.then_inc(f_ok, 1)
                run_steps(pe, PAIRS, 2, body)

            @block.scalar
            def _(act):
                def body(g, u, live):
                    if live(0):
                        act.wait_ge(t_ok, g + 1)
                        if is_later(g, 2):
                            act.wait_ge(f_ok, g - 1)
                        nc.scalar.copy(x3t[:, u, :], ps_t[:, u, 0:2 * P]).then_inc(xt_ok, 1)
                    if live(2):
                        act.wait_ge(rfs_ok, g - 1)
                        nc.scalar.copy(duo(rf_all, g - 2), rfs[:, u, :]).then_inc(rf_ok, 1)
                    if live(1):
                        j, v = g - 1, 1 - u
                        act.wait_ge(f_ok, j + 1)
                        if is_later(j, 2):
                            act.wait_ge(q_ok, j - 1)
                            act.wait_ge(rf_ok, j - 1)
                        nc.scalar.copy(rfs[:, v, :], ps_f[:, v, 0:2 * P]).then_inc(rfs_ok, 1)
                run_steps(act, PAIRS, 2, body)

            @block.vector
            def _(dve):
                def body(g, u, live):
                    if live(0):
                        if is_later(g, 2):
                            dve.wait_ge(t_ok, g - 1)
                            dve.wait_ge(cp_ok, g - 1)
                        normalise2(x3[:, u, :], g).then_inc(n_ok, 1)
                    if live(1):
                        j, v = g - 1, 1 - u
                        dve.wait_ge(sq_ok, j + 1)
                        nc.vector.tensor_tensor(a2_part(j, 0), a2[:, v, :], a2[:, v, :], ALU.max).then_inc(hi_ok, 1)
                    if live(3):
                        i = g - 3
                        dve.wait_ge(q_ok, i + 1)
                        nc.vector.tensor_scalar(duo(y_all, i), ps_q[:, 1 - u, 0:2 * P], col[:, C_B2:C_B2 + 1], None, ALU.mult).then_inc(y_ok, 1)
                    if live(1):
                        dve.wait_ge(hi_ok, j + 1)
                        nc.vector.tensor_tensor(a2_part(j, 1), a2[:, v, :], a2_part(j, 0), ALU.subtract).then_inc(lo_ok, 1)
                run_steps(dve, PAIRS, 3, body)

        GAUSS, FIRST, LN, SECOND, GATHER = 1, 3, 4, 5, 6
        EARLY = 2
        HG = GPB // 2
        with ExitStack() as cx, nc.Block() as block:
            def tmp(name, shape, dt=F32):
                return cx.enter_context(nc.sbuf_tensor("l3_" + name, shape, dt))

            e_ring = tmp("e_ring", [6, 2, HG * 512], BF16)
            dist2 = tmp("dist2", [P, 2, 512])
            WORK = 8192
            work = big[:, 2 * B * P:2 * B * P + WORK] if B * P >= WORK else tmp("work", [P, WORK])[:, :]
            ex, h, zt = (work[:, n * 2048:(n + 1) * 2048].rearrange("p (u c) -> p u c", u=2) for n in range(3))
            gauss = work[:, 6144:7168].rearrange("p (u c) -> p u c", u=2)
            zl = work[:, 7168:8192].bitcast(BF16).rearrange("p (u c) -> p u c", u=2)
            z_upper = work[:, 4096:6144].bitcast(BF16).rearrange("p (u c t) -> p u c t", u=2, t=2)[:, :, :, 1]
            g_upper = work[:, 6144:7168].bitcast(BF16).rearrange("p (u c t) -> p u c t", u=2, t=2)[:, :, :, 1]
            gl = tmp("gl", [P, 2, 512], BF16)
            a2_half = tmp("a2_half", [P, HG * ROWS])
            a2_now = a2_half[:, :].bitcast(BF16)
            ps_e = cx.enter_context(nc.psum_tensor("l3_ps_e", [P, 512], F32))
            ps_v = cx.enter_context(nc.psum_tensor("l3_ps_v", [P, 2, 1024], F32))
            ps_w = cx.enter_context(nc.psum_tensor("l3_ps_w", [P, 2, 512], F32))
            w_all = ps_w[:, :, :].rearrange("p h c -> p (h c)")
            ps_y = cx.enter_context(nc.psum_tensor("l3_ps_y", [P, 512], F32))
            (e_mm, sq_ok, g_ok, gl_ok, v_mm, ev_ok, cap_ok, ln_ok, h_ok, w_mm, z_ok, zl_ok, y_mm, y_half, y_ev, a2_in) = (
                cx.enter_context(nc.semaphore("l3_" + n))
                for n in ("e_mm", "sq_ok", "g_ok", "gl_ok", "v_mm", "ev_ok", "cap_ok", "ln_ok", "h_ok", "w_mm", "z_ok", "zl_ok", "y_mm",
                          "y_half", "y_ev", "a2_in"))
            e_in = [cx.enter_context(nc.semaphore(f"l3_e_in{u}")) for u in range(2)]

            def back(b, s, lag):
                c, r = (b, s - lag) if s >= lag else (b - 1, s - lag + GPB)
                return c, r, c * GPB + r

            def all_groups(eng, step):
                for s in range(GPB):
                    step(0, s, lambda lag: s - lag >= 0)
                with eng.Fori(1, B) as b:
                    for s in range(GPB):
                        step(b, s, lambda lag: True)
                for s in range(GATHER):
                    step(B, s, lambda lag: s < lag)

            @block.sync
            def _(sp):
                def load(b):
                    for side in range(2):
                        if is_later(b, 1):
                            sp.wait_ge(e_mm, (b - 1) * GPB + (side + 1) * HG)
                        for part in range(3):
                            src = parts[part, b] if isinstance(b, int) else parts[part, bass.ds(b, 1)].rearrange("o i j -> (o i) j")
                            src = src[side * HG * ROWS:(side + 1) * HG * ROWS]
                            sp.dma_start(e_ring[2 * part:2 * part + 2, side, :].rearrange("h (s c) -> h s c", c=512),
                                         src.rearrange("(s h r) j -> h s (r j)", h=2, r=HALF)).then_inc(e_in[side], 16)
                load(0)
                with sp.Fori(1, B) as b:
                    load(sp.snap(b))

            @block.tensor
            def _(pe):
                def spread(b, s, k):
                    if s % HG == 0:
                        pe.wait_ge(e_in[s // HG], 48 * (b + 1))
                    if is_later(k, 1):
                        pe.wait_ge(sq_ok, k)
                    nc.tensor.matmul(ps_e[:, :], half[:, :], e_ring[:, s // HG, s % HG * 512:(s % HG + 1) * 512],
                                     start=True, stop=True).then_inc(e_mm, 1)

                def first(k, u):
                    pe.wait_ge(gl_ok, k + 1)
                    if is_later(k, 2):
                        pe.wait_ge(h_ok, k - 1)
                    for side in range(2):
                        half_p = slice(side * NG, (side + 1) * NG)
                        v = ps_v[:, u, side * 512:(side + 1) * 512]
                        nc.tensor.matmul(v, w1_hi[half_p, :], g_upper[half_p, u, :], start=True, stop=False)
                        nc.tensor.matmul(v, w1_hi[half_p, :], gl[half_p, u, :], start=False, stop=False)
                        last = nc.tensor.matmul(v, w1_lo[half_p, :], g_upper[half_p, u, :], start=False, stop=True)
                    last.then_inc(v_mm, 1)

                def second(k, u):
                    pe.wait_ge(h_ok, k + 1)
                    for side in range(2):
                        if is_later(k, 1):
                            pe.wait_ge(z_ok, 3 * k - 1 + side)
                        for i in range(HALF):
                            c = (side * HALF + i) * P
                            last = nc.tensor.matmul(ps_w[:, side, i * P:(i + 1) * P], h[:, u, c:c + P], wt[:, W2T, :],
                                                    start=True, stop=True)
                        last.then_inc(w_mm, 1)

                def gather(b, s, k, u):
                    if s % HG == 0:
                        pe.wait_ge(a2_in, 2 * b + s // HG + 1)
                        if is_later(k, 1):
                            pe.wait_ge(y_ev, 2 * b + s // HG)
                    pe.wait_ge(zl_ok, k + 1)
                    for i in range(ROWS):
                        at_y = (s % HG * ROWS + i) * 2
                        nc.tensor.matmul(ps_y[:, at_y:at_y + 2], z_upper[:, u, i * P:(i + 1) * P], a2_now[:, at_y:at_y + 2],
                                         start=True, stop=False)
                        last = nc.tensor.matmul(ps_y[:, at_y:at_y + 2], zl[:, u, i * P:(i + 1) * P], a2_now[:, at_y:at_y + 2],
                                                start=False, stop=True)
                    last.then_inc(y_mm, 1)

                def step(b, s, live):
                    if live(FIRST):
                        first(back(b, s, FIRST)[2], (s - FIRST) % 2)
                    if live(SECOND):
                        second(back(b, s, SECOND)[2], (s - SECOND) % 2)
                    if live(GATHER):
                        gather(*back(b, s, GATHER), (s - GATHER) % 2)
                    if live(0):
                        spread(*back(b, s, 0))
                all_groups(pe, step)

            @block.gpsimd
            def _(pool):
                def step(b, s, live):
                    if live(GATHER):
                        j, u = back(b, s, GATHER)[2], (s - GATHER) % 2
                        pool.wait_ge(z_ok, 3 * j + 3)
                        if is_later(j, 2):
                            pool.wait_ge(y_mm, j - 1)
                        nc.gpsimd.tensor_tensor(zl[:, u, :], zt[:, u, :], z_upper[:, u, :], ALU.subtract).then_inc(zl_ok, 1)
                    if live(GAUSS):
                        k, u = back(b, s, GAUSS)[2], (s - GAUSS) % 2
                        pool.wait_ge(g_ok, k + 1)
                        if is_later(k, 2):
                            pool.wait_ge(v_mm, k - 1)
                        nc.gpsimd.tensor_tensor(gl[:, u, :], gauss[:, u, :], g_upper[:, u, :], ALU.subtract).then_inc(gl_ok, 1)
                all_groups(pool, step)

            @block.scalar
            def _(act):
                def step(b, s, live):
                    if live(LN):
                        j, u = back(b, s, LN)[2], (s - LN) % 2
                        act.wait_ge(cap_ok, j + 1)
                        nc.scalar.activation(ex[:, u, :], ex[:, u, :], ACT.Ln, scale=0.5, bias=0.5).then_inc(ln_ok, 1)
                    if live(GAUSS):
                        k, v = back(b, s, GAUSS)[2], (s - GAUSS) % 2
                        act.wait_ge(e_mm, k + 1)
                        nc.scalar.activation(dist2[:, v, :], ps_e[:, :], ACT.Square, bias=col[:, C_NOFF:C_NOFF + 1]).then_inc(sq_ok, 1)
                    if live(FIRST):
                        j, u = back(b, s, FIRST)[2], (s - FIRST) % 2
                        act.wait_ge(v_mm, j + 1)
                        if is_later(j, 2):
                            act.wait_ge(h_ok, j - 1)
                        nc.scalar.activation(ex[:, u, :], ps_v[:, u, :], ACT.Exp, bias=col[:, C_B1:C_B1 + 1]).then_inc(ev_ok, 1)
                    if live(GAUSS):
                        k, v = back(b, s, GAUSS)[2], (s - GAUSS) % 2
                        act.wait_ge(sq_ok, k + 1)
                        if is_later(k, 2):
                            act.wait_ge(v_mm, k - 1)
                        nc.scalar.activation(gauss[:, v, :], dist2[:, v, :], ACT.Exp, scale=coeff).then_inc(g_ok, 1)
                nc.scalar.preload_act_table_set("natural_log_exp_and_others")
                all_groups(act, step)

            @block.vector
            def _(dve):
                def evacuate(b, side):
                    dve.wait_ge(y_mm, b * GPB + (side + 1) * HG)
                    start = b * P + side * HG * ROWS
                    y = y_all[:, start:start + HG * ROWS] if isinstance(start, int) else y_all[:, bass.ds(start, HG * ROWS)]
                    y2 = ps_y[:, 0:2 * HG * ROWS].rearrange("p (c t) -> p t c", t=2)
                    nc.vector.tensor_tensor(y, y2[:, 0, :], y, ALU.add).then_inc(y_half, 1)
                    dve.wait_ge(y_half, 2 * b + side + 1)
                    nc.vector.tensor_tensor(y, y2[:, 1, :], y, ALU.add).then_inc(y_ev, 1)

                def fetch_a2(b, side):
                    start = b * P + side * HG * ROWS
                    src = adj_t[:, start:start + HG * ROWS] if isinstance(start, int) else adj_t[:, bass.ds(start, HG * ROWS)]
                    nc.vector.tensor_copy(a2_half[:, :], src).then_inc(a2_in, 1)

                def weigh(b, s, k, rows, side):
                    u, n = s % 2, rows.stop - rows.start
                    cols = slice(rows.start * P, rows.stop * P)
                    rf = at(rf_all, b).unsqueeze(1).to_broadcast([P, n, P])
                    dve.wait_ge(w_mm, 2 * k + 1 + side)
                    if rows.start == 0 and is_later(k, 2):
                        dve.wait_ge(y_mm, k - 1)
                        dve.wait_ge(zl_ok, k - 1)
                    nc.vector.tensor_tensor(zt[:, u, cols].rearrange("p (i f) -> p i f", f=P),
                                            w_all[:, cols].rearrange("p (i f) -> p i f", f=P), rf, ALU.mult).then_inc(z_ok, 1)

                def step(b, s, live):
                    if s == GATHER:
                        if is_later(b, 1):
                            evacuate(b - 1, 1)
                        fetch_a2(b, 0)
                    if s == GATHER + HG:
                        evacuate(b, 0)
                        fetch_a2(b, 1)
                    if live(LN):
                        j, u = back(b, s, LN)[2], (s - LN) % 2
                        dve.wait_ge(ln_ok, j + 1)
                        if is_later(j, 2):
                            dve.wait_ge(w_mm, 2 * (j - 1))
                        nc.vector.scalar_tensor_tensor(h[:, u, :], ps_v[:, u, :], b1_ln2[:, 0:1], ex[:, u, :],
                                                       ALU.add, ALU.max).then_inc(h_ok, 1)
                    if live(SECOND):
                        weigh(*back(b, s, SECOND), slice(0, EARLY), 0)
                    if live(FIRST):
                        j, u = back(b, s, FIRST)[2], (s - FIRST) % 2
                        dve.wait_ge(ev_ok, j + 1)
                        nc.vector.tensor_scalar_min(ex[:, u, :], ex[:, u, :], EXP_CAP).then_inc(cap_ok, 1)
                    if live(SECOND):
                        weigh(*back(b, s, SECOND), slice(EARLY, HALF), 0)
                        weigh(*back(b, s, SECOND), slice(HALF, ROWS), 1)
                all_groups(dve, step)
                evacuate(B - 1, 1)

        Q = 4
        CHUNKS = B // Q
        with ExitStack() as cx, nc.Block() as block:
            def tmp(name, shape, dt=F32):
                return cx.enter_context(nc.sbuf_tensor("l3e_" + name, shape, dt))

            def ps(name):
                return cx.enter_context(nc.psum_tensor("l3e_" + name, [P, 2, 512], F32))

            ex, s, t_o = (tmp(n, [P, 2, Q * P]) for n in ("ex", "s", "t"))
            ps_d, ps_o = ps("ps_d"), ps("ps_o")
            d_mm, ev_ok, cap_ok, ln_ok, s_ok, o_mm, t_ok, r_ok = (
                cx.enter_context(nc.semaphore("l3e_" + n))
                for n in ("d_mm", "ev_ok", "cap_ok", "ln_ok", "s_ok", "o_mm", "t_ok", "r_ok"))

            @block.tensor
            def _(pe):
                for c in range(CHUNKS + 1):
                    if c < CHUNKS:
                        if c >= 2:
                            pe.wait_ge(s_ok, c - 1)
                        nc.tensor.matmul(ps_d[:, c % 2, :], wt[:, WD1T, :], y_all[:, c * Q * P:(c + 1) * Q * P],
                                         start=True, stop=True).then_inc(d_mm, 1)
                    if c >= 1:
                        j, v = c - 1, (c - 1) % 2
                        pe.wait_ge(s_ok, j + 1)
                        if j >= 2:
                            pe.wait_ge(t_ok, j - 1)
                        for q in range(Q):
                            last = nc.tensor.matmul(ps_o[:, v, q * P:(q + 1) * P], s[:, v, q * P:(q + 1) * P], wt[:, WD2T, :],
                                                    start=True, stop=True)
                        last.then_inc(o_mm, 1)

            @block.scalar
            def _(act):
                for c in range(CHUNKS + 1):
                    if c < CHUNKS:
                        u = c % 2
                        act.wait_ge(d_mm, c + 1)
                        if c >= 2:
                            act.wait_ge(s_ok, c - 1)
                        nc.scalar.activation(ex[:, u, :], ps_d[:, u, :], ACT.Exp, bias=col[:, C_BD1:C_BD1 + 1]).then_inc(ev_ok, 1)
                    if c >= 1:
                        v = (c - 1) % 2
                        act.wait_ge(cap_ok, c)
                        nc.scalar.activation(ex[:, v, :], ex[:, v, :], ACT.Ln, scale=0.5, bias=0.5).then_inc(ln_ok, 1)

            @block.vector
            def _(dve):
                for c in range(CHUNKS + 3):
                    if c < CHUNKS:
                        dve.wait_ge(ev_ok, c + 1)
                        nc.vector.tensor_scalar_min(ex[:, c % 2, :], ex[:, c % 2, :], EXP_CAP).then_inc(cap_ok, 1)
                    if 2 <= c < CHUNKS + 2:
                        j, u = c - 2, c % 2
                        dve.wait_ge(o_mm, j + 1)
                        chunk = x_all[:, j * Q * P:(j + 1) * Q * P].rearrange("p (q e) -> p q e", e=P)
                        to3 = t_o[:, u, :].rearrange("p (q e) -> p q e", e=P)
                        nc.vector.tensor_tensor(to3, ps_o[:, u, :].rearrange("p (q e) -> p q e", e=P),
                                                row[:, R_BD2, :].unsqueeze(1).to_broadcast([P, Q, P]), ALU.add).then_inc(t_ok, 1)
                    if 1 <= c < CHUNKS + 1:
                        i, v = c - 1, (c - 1) % 2
                        dve.wait_ge(ln_ok, i + 1)
                        if i >= 2:
                            dve.wait_ge(o_mm, i - 1)
                        nc.vector.scalar_tensor_tensor(s[:, v, :], ps_d[:, v, :], bd1_ln2[:, 0:1], ex[:, v, :],
                                                       ALU.add, ALU.max).then_inc(s_ok, 1)
                    if 2 <= c < CHUNKS + 2:
                        dve.wait_ge(t_ok, j + 1)
                        nc.vector.tensor_tensor(chunk, to3, chunk, ALU.add).then_inc(r_ok, 1)
                    if c >= 3:
                        dve.wait_ge(r_ok, c - 2)
                        for q in range(Q):
                            row_stats((c - 3) * Q + q)

        rstd_phase("ln3")

        with ExitStack() as cx, nc.Block() as block:
            n_ok = cx.enter_context(nc.semaphore("out_n_ok"))
            stored = cx.enter_context(nc.semaphore("stored"))

            @block.vector
            def _(dve):
                with dve.Fori(0, CHUNKS) as c:
                    x, m, rs = (t[:, bass.ds(c * n, n)] for t, n in ((x_all, Q * P), (mean, Q), (rstd, Q)))
                    for q in range(Q):
                        xq = x[:, q * P:(q + 1) * P]
                        nc.vector.tensor_scalar(xq, xq, m[:, q:q + 1], rs[:, q:q + 1], ALU.subtract, ALU.mult).then_inc(n_ok, 1)

            @block.sync
            def _(sp):
                for c in range(B // Q):
                    sp.wait_ge(n_ok, (c + 1) * Q)
                    sp.dma_start(out[c * Q:(c + 1) * Q].rearrange("b n d -> n b d"),
                                 x_all[:, c * Q * P:(c + 1) * Q * P].rearrange("p (b d) -> p b d", d=P)).then_inc(stored, 16)
                sp.wait_ge(stored, 16 * (B // Q))


def kernel(**inputs):
    import numpy as _np
    import concourse.bacc as _bacc
    from concourse import mybir as _mybir
    from concourse.bass_utils import run_bass_kernel_spmd as _run

    g = {n: _np.asarray(a) for n, a in inputs.items()}
    n_graphs = g["x"].shape[0]
    eye = _np.eye(P, dtype=_np.float32)
    off = _np.linspace(0.0, CUTOFF, NG, dtype=_np.float32)
    neg_offsets = _np.concatenate([-off, -off])
    side_of_row = _np.tile(_np.repeat(_np.eye(2, dtype=_np.float32), P // 2, axis=1), (3, 1))
    l1 = {n[len("L1_gnn_"):]: a for n, a in g.items() if n.startswith("L1_gnn_")}
    l3 = {n[len("L3_gnn_"):]: a for n, a in g.items() if n.startswith("L3_gnn_")}
    host = {
        "x": g["x"],
        "adj": g["adj"],
        "adjt": g["adj"].transpose(0, 2, 1),
        "weights": _np.stack([g["L0_gnn_W"].T, l1["W_ir"], l1["W_iz"], l1["W_im"], l1["W_xr"], l1["W_xz"], l1["W_xm"],
                              l1["W_hr"], l1["W_hz"], l1["W_hm"], g["L2_gnn_theta"], l3["Wa"].T, l3["W2"].T,
                              l3["Wd1"].T, l3["Wd2"].T, eye, 1 - eye], axis=1),
        "w1t": l3["W1"].T,
        "columns": _np.stack([l1["b_xr"], l1["b_hr"], l1["b_xz"], l1["b_hz"], l1["b_xm"], l1["b_hm"],
                              l3["b1"], l3["b2"], l3["bd1"], neg_offsets], axis=1),
        "rows": _np.stack([g["L0_gnn_b"], l1["b_ir"], l1["b_iz"], l1["b_im"], g["L2_gnn_bias"], l3["bd2"]], axis=0),
        "halves": side_of_row,
    }
    nc = _bacc.Bacc("TRN2", target_bir_lowering=False, num_devices=1)
    arrays, args = {}, []
    for name, a in host.items():
        a = _np.ascontiguousarray(a)
        arrays[f"in_{name}_dram"] = a
        args.append(nc.dram_tensor(f"in_{name}_dram", a.shape, _mybir.dt.from_np(a.dtype), kind="ExternalInput").ap())
    out = nc.dram_tensor("out_dram", g["x"].shape, _mybir.dt.float32, kind="ExternalOutput").ap()
    parts = nc.dram_tensor("adj_parts_dram", (3, n_graphs, P, P), _mybir.dt.bfloat16).ap()
    build(nc, n_graphs, *args, out, parts)
    r = _run(nc, [arrays], core_ids=[0])
    return r.results[0]["out_dram"]
```
